# Optimizing a Trainium2 kernel written in Bass

```python
import numpy as np
import jax
import jax.numpy as jnp

def _softmax(x, axis=-1):
    return jax.nn.softmax(x, axis=axis)

def _gelu(x):
    return jax.nn.gelu(x, approximate=True)

def _silu(x):
    return jax.nn.silu(x)

def _sigmoid(x):
    return jax.nn.sigmoid(x)

def _layernorm(x, axis=-1, eps=1e-05):
    m = jnp.mean(x, axis=axis, keepdims=True)
    v = jnp.var(x, axis=axis, keepdims=True)
    return (x - m) / jnp.sqrt(v + eps)

def _scatter_add(tgt, idx, src, axis=0):
    return tgt.at[idx].add(src)

def _segment_sum(src, seg, n):
    return jax.ops.segment_sum(src, seg, n)
kernel_name = 'mk_early_fusion_d1_tok_img1024_r4_9fe0ab'

def setup_inputs(seed: int=0):
    np.random.seed(seed)
    _w = jnp.asarray

    def _rec_inputs():
        import jax
        import jax.numpy as jnp
        _rk = jax.random.key(seed)
        x = -0.000356955 + 1 * jax.random.normal(jax.random.fold_in(_rk, 1), (64, 3, 224, 224), jnp.float32)
        txt = -0.000394971 + 1.15376 * jax.random.normal(jax.random.fold_in(_rk, 2), (64, 32, 256), jnp.float32)
        return (x, txt)
    x, txt = _rec_inputs()

    def _L0_tok_setup():
        import jax, jax.numpy as jnp
        import numpy as np
        PATCH = 16
        H = W = 224
        C = 3
        NP_SIDE = H // PATCH
        NUM_PATCHES = NP_SIDE * NP_SIDE
        PATCH_DIM = C * PATCH * PATCH
        EMBED = 256
        key = jax.random.key(seed)
        k1, k2, k3, k4 = jax.random.split(key, 4)
        B = 128
        raw_pixels = jax.random.normal(k1, (B, C, H, W), dtype=jnp.float32)
        bound = 1.0 / np.sqrt(PATCH_DIM)
        W_embed = jax.random.uniform(k2, (PATCH_DIM, EMBED), minval=-bound, maxval=bound, dtype=jnp.float32)
        b_embed = jax.random.uniform(k3, (EMBED,), minval=-bound, maxval=bound, dtype=jnp.float32)
        pos_embed = jax.random.normal(k4, (1, NUM_PATCHES, EMBED), dtype=jnp.float32)
        return {'raw_pixels': raw_pixels, 'W_embed': W_embed, 'b_embed': b_embed, 'pos_embed': pos_embed}
    _L0_tok_all = _L0_tok_setup()
    _L0_tok_in = {k: v for k, v in _L0_tok_all.items() if k in ('W_embed', 'b_embed', 'pos_embed')}
    del _L0_tok_all

    def _L0_attn_setup():
        import jax, jax.numpy as jnp
        import numpy as np
        NUM_HEADS = 16
        key = jax.random.key(seed)
        ks = jax.random.split(key, 6)
        B, S, D = (2, 512, 256)
        x = jax.random.normal(ks[0], (B, S, D), dtype=jnp.float32)
        scale = 0.02
        Wq = jax.random.normal(ks[1], (D, D), dtype=jnp.float32) * scale
        Wk = jax.random.normal(ks[2], (D, D), dtype=jnp.float32) * scale
        Wv = jax.random.normal(ks[3], (D, D), dtype=jnp.float32) * scale
        Wo = jax.random.normal(ks[4], (D, D), dtype=jnp.float32) * scale
        bo = jax.random.normal(ks[5], (D,), dtype=jnp.float32) * scale
        return {'x': x, 'Wq': Wq, 'Wk': Wk, 'Wv': Wv, 'Wo': Wo, 'bo': bo}
    _L0_attn_all = _L0_attn_setup()
    _L0_attn_in = {k: v for k, v in _L0_attn_all.items() if k in ('Wq', 'Wk', 'Wv', 'Wo', 'bo')}
    del _L0_attn_all

    def _L0_ffn_setup():
        import jax, jax.numpy as jnp
        import numpy as np
        EPS = 1e-08

        def _ternary_linear(x, w):
            alpha = jnp.mean(jnp.abs(w))
            w_t = jnp.sign(w) * (jnp.abs(w) > 0.5 * alpha).astype(w.dtype)
            w_q = w + jax.lax.stop_gradient(w_t - w)
            d = x.shape[-1]
            rms = jnp.sqrt(jnp.sum(x * x, axis=-1, keepdims=True)) / jnp.sqrt(jnp.asarray(d, x.dtype))
            x_norm = x / (rms + EPS)
            return jnp.einsum('bsd,fd->bsf', x_norm, w_q)
        key = jax.random.key(seed)
        k1, k2, k3 = jax.random.split(key, 3)
        d_model, d_ff = (256, 1024)
        B, S = (4, 1024)
        x = jax.random.normal(k1, (B, S, d_model), dtype=jnp.float32)
        w_up = jax.random.normal(k2, (d_ff, d_model), dtype=jnp.float32) * 0.02
        w_down = jax.random.normal(k3, (d_model, d_ff), dtype=jnp.float32) * 0.02
        return {'x': x, 'w_up': w_up, 'w_down': w_down}
    _L0_ffn_all = _L0_ffn_setup()
    _L0_ffn_in = {k: v for k, v in _L0_ffn_all.items() if k in ('w_up', 'w_down')}
    del _L0_ffn_all
    return {'x': x, 'txt': txt, 'L0_tok_W_embed': _L0_tok_in['W_embed'], 'L0_tok_b_embed': _L0_tok_in['b_embed'], 'L0_tok_pos_embed': _L0_tok_in['pos_embed'], 'L0_attn_Wq': _L0_attn_in['Wq'], 'L0_attn_Wk': _L0_attn_in['Wk'], 'L0_attn_Wv': _L0_attn_in['Wv'], 'L0_attn_Wo': _L0_attn_in['Wo'], 'L0_attn_bo': _L0_attn_in['bo'], 'L0_ffn_w_up': _L0_ffn_in['w_up'], 'L0_ffn_w_down': _L0_ffn_in['w_down']}

def reference(x, txt, L0_tok_W_embed, L0_tok_b_embed, L0_tok_pos_embed, L0_attn_Wq, L0_attn_Wk, L0_attn_Wv, L0_attn_Wo, L0_attn_bo, L0_ffn_w_up, L0_ffn_w_down):
    import jax
    import jax.numpy as jnp

    def _L0_tok_ref(raw_pixels, W_embed, b_embed, pos_embed):
        import jax, jax.numpy as jnp
        import numpy as np
        PATCH = 16
        H = W = 224
        C = 3
        NP_SIDE = H // PATCH
        NUM_PATCHES = NP_SIDE * NP_SIDE
        PATCH_DIM = C * PATCH * PATCH
        EMBED = 256
        B = raw_pixels.shape[0]
        patches = raw_pixels.reshape(B, C, NP_SIDE, PATCH, NP_SIDE, PATCH)
        patches = patches.transpose(0, 2, 4, 1, 3, 5).reshape(B, NUM_PATCHES, PATCH_DIM)
        x = jnp.einsum('bnd,de->bne', patches, W_embed) + b_embed
        return x + pos_embed

    def _L0_attn_ref(x, Wq, Wk, Wv, Wo, bo):
        import jax, jax.numpy as jnp
        import numpy as np
        NUM_HEADS = 16
        B, S, D = x.shape
        H = NUM_HEADS
        hd = D // H
        q = (x @ Wq.T).reshape(B, S, H, hd).transpose(0, 2, 1, 3)
        k = (x @ Wk.T).reshape(B, S, H, hd).transpose(0, 2, 1, 3)
        v = (x @ Wv.T).reshape(B, S, H, hd).transpose(0, 2, 1, 3)
        scores = jnp.einsum('bhqd,bhkd->bhqk', q, k) / jnp.sqrt(jnp.float32(hd))
        causal = jnp.triu(jnp.ones((S, S), dtype=bool), k=1)
        scores = jnp.where(causal, -jnp.inf, scores)
        probs = jax.nn.softmax(scores, axis=-1)
        ctx = jnp.einsum('bhqk,bhkd->bhqd', probs, v)
        ctx = ctx.transpose(0, 2, 1, 3).reshape(B, S, D)
        return ctx @ Wo.T + bo

    def _L0_ffn_ref(x, w_up, w_down):
        import jax, jax.numpy as jnp
        import numpy as np
        EPS = 1e-08

        def _ternary_linear(x, w):
            alpha = jnp.mean(jnp.abs(w))
            w_t = jnp.sign(w) * (jnp.abs(w) > 0.5 * alpha).astype(w.dtype)
            w_q = w + jax.lax.stop_gradient(w_t - w)
            d = x.shape[-1]
            rms = jnp.sqrt(jnp.sum(x * x, axis=-1, keepdims=True)) / jnp.sqrt(jnp.asarray(d, x.dtype))
            x_norm = x / (rms + EPS)
            return jnp.einsum('bsd,fd->bsf', x_norm, w_q)
        h = jax.nn.gelu(_ternary_linear(x, w_up), approximate=False)
        return _ternary_linear(h, w_down)
    h = _L0_tok_ref(x, L0_tok_W_embed, L0_tok_b_embed, L0_tok_pos_embed)
    h = jnp.concatenate([h, txt], axis=1)
    h = h + _L0_attn_ref(_layernorm(h, axis=-1), L0_attn_Wq, L0_attn_Wk, L0_attn_Wv, L0_attn_Wo, L0_attn_bo)
    h = h + _L0_ffn_ref(_layernorm(h, axis=-1), L0_ffn_w_up, L0_ffn_w_down)
    return h

_drawn_inputs = setup_inputs


def setup_inputs(seed=0):
    import zlib

    import numpy as np

    out = dict(_drawn_inputs(seed))
    spreads = {}
    factors = {'L0_tok_b_embed': 3.03,
     'L0_attn_Wq': 8.0,
     'L0_attn_Wk': 8.0,
     'L0_attn_Wv': 3.205,
     'L0_attn_Wo': 2.934,
     'L0_attn_bo': 3.027}
    for name, (base, spread) in spreads.items():
        noise = np.random.default_rng([zlib.crc32(name.encode()), seed]).standard_normal(out[name].shape)
        drawn = base * np.exp(spread * noise) if base else spread * noise
        out[name] = jnp.asarray(drawn.astype(out[name].dtype))
    for name, factor in factors.items():
        out[name] = (out[name] * factor).astype(out[name].dtype)
    return out
```

```python
from contextlib import ExitStack

import numpy as np
import concourse.bass as bass
from concourse import mybir

ALU = mybir.AluOpType
ACT = mybir.ActivationFunctionType
AX = mybir.AxisListType
F32 = mybir.dt.float32
F32R = mybir.dt.float32r
F16 = mybir.dt.float16
BF16 = mybir.dt.bfloat16

B, C, SIDE, PATCH = 64, 3, 224, 16
NS = SIDE // PATCH
NPATCH = NS * NS
TXT = 32
S = NPATCH + TXT
R = S // 2
RP1 = NPATCH - R
D, H, HD, FF = 256, 16, 16, 1024
NPAIR = B // 2
T2 = 2 * S
TP = 2 * NPATCH
PROWS = 2 * C * NS
PCOLS = PATCH * SIDE
NFF = FF // 128
NXG = [(0, 5), (5, 10), (10, 14)]
HS = H * S
PAD = 16
VW = 1 + 3 * HD
PARTS = [(0, 0), (0, 1), (0, 2), (1, 0), (1, 1), (2, 0)]
KS = len(PARTS) * HD
KM = KS + 3
EPS = 1e-5
RMS_EPS = 1e-8
NEG = -1e30

DENSE = [("pix", k) for k in range(6)] + [("emb", 0), ("emb", 1), ("ct", 0), ("ct", 1),
         ("up", 0), ("up", 1), ("o", 0), ("o", 1), ("ht", 0), ("ht", 1), ("up", 2), ("up", 3),
         ("up", 4), ("up", 5), ("xt", 0), ("xt", 1), ("up", 6), ("up", 7), ("qk", 0), ("qk", 1),
         ("qk", 2), ("qk", 3), ("v", 0), ("v", 1), ("ss", 0), ("dn", 0), ("dn", 1), ("x2t", 0),
         ("x2t", 1)]
DENSE.insert(8, ("spare", 0))
PER = {"pix": 6, "emb": 2, "ct": 2, "up": 8, "o": 2, "ht": 2, "xt": 2, "qk": 4, "v": 2, "ss": 1,
       "dn": 2, "x2t": 2}
LAG = {"pix": 0, "emb": 0, "ht": 0, "xt": 0, "qk": 0, "v": 0, "ct": 2, "o": 2, "x2t": 2, "up": 3,
       "ss": 3, "dn": 3}
NDENSE = len(DENSE)
assert NDENSE % 3 == 0


def build(nc, x, txt, w_embed, b_embed, pos, wqkvo, bo, w_upT, w_downT, out):
    qk_scr = nc.dram_tensor("qk_scr", (2, 2, 2, 3, 2, 128, S), BF16, kind="Internal").ap()
    m_scr = nc.dram_tensor("m_scr", (2, 2, 48, S), BF16, kind="Internal").ap()

    with ExitStack() as ctx:
        def sb(name, shape, dt):
            return ctx.enter_context(nc.sbuf_tensor(name, shape, dt))

        def sem(name):
            return ctx.enter_context(nc.semaphore(name))

        ident = sb("ident", [128, 128], F32)
        identb = sb("identb", [128, 128], BF16)
        cmask = sb("cmask", [128, R], BF16)
        onesb = sb("onesb", [128, 2], BF16)
        posb = sb("posb", [R, 2, D], F32)
        borow = sb("borow", [R, D], F32)
        we = [sb("we_hi", [128, 6, D], F32R), sb("we_lo", [128, 6, D], F32R)]
        wa = [sb("wa_hi", [128, 4, 2, D], F32R), sb("wa_lo", [128, 4, 2, D], F32R)]
        wup = sb("wup", [128, 2, FF], BF16)
        wdn = sb("wdn", [128, NFF, D], BF16)
        tern = sb("tern", [128, 8], F32)
        pix = sb("pix", [PROWS, PCOLS], F32)
        pT = [sb("pT_hi", [128, 2, 2 * C * NPATCH], F32R), sb("pT_lo", [128, 2, 2 * C * NPATCH], F32R)]
        hT = sb("hT", [128, 2, TP], F32)
        h = sb("h", [128, 2, 4 * D], F32)
        st1 = sb("st1", [R, 4, 6], F32)
        mv1 = sb("mv1", [R, 4, 2], F32)
        rstd1 = sb("rstd1", [R, 2, 4], F32)
        exps = sb("exps", [R, 3, 4], F32)
        aT = [sb("aT_hi", [128, 2, T2], F32R), sb("aT_lo", [128, 2, T2], F32R)]
        qkp = sb("qkp", [128, 2, 3, T2], BF16)
        qkr = sb("qkr", [128, T2], F32)
        vp = sb("vp", [R, 2, 4, H, VW], BF16)
        vr = sb("vr", [R, 2 * D], F32)
        qst = [sb(f"qst{b}", [KM, HS + PAD], BF16) for b in range(2)]
        kst = [sb(f"kst{b}", [KM, HS + PAD], BF16) for b in range(2)]
        mx = sb("mx", [R, 2, 2, H], F32)
        mr = sb("mr", [R, 2, 2, H], F32)
        mp = sb("mp", [R, 2, 2, 3, H], BF16)
        mT = sb("mT", [48, 2, S], BF16)
        PW = 3 * T2 + PAD
        pr = [sb(f"pr{i}", [R, PW], F32) for i in range(2)]
        pl = [sb(f"pl{i}", [R, PW], F16) for i in range(2)]
        cu = sb("cu", [R, 2, 8, HD], F32)
        rs = sb("rs", [R, 2, 8], F32)
        cx = sb("cx", [R, 4, D], F32)
        xn = cx[:].rearrange("p j d -> p (j d)")
        h2 = sb("h2", [128, 2, 4 * D], F32)
        xn2 = sb("xn2", [R, 4 * D], F32)
        st2 = sb("st2", [R, 4, 6], F32)
        mv2 = sb("mv2", [R, 4, 2], F32)
        ln2 = sb("ln2", [R, 7, 4], F32)
        xT2 = [sb("xT2_hi", [128, 2, T2], F16), sb("xT2_lo", [128, 2, T2], F16)]
        g = sb("g", [128, NFF, T2], F32)
        gl = sb("gl", [128, NFF, T2], F16)
        sq = sb("sq", [128, 2, T2], F32)
        acc = sb("acc", [128, T2], F32)
        accl = sb("accl", [128, T2], F16)
        ssq = sb("ssq", [R, 4, 4], F32)
        patches = g[0:PROWS].rearrange("p a b -> p (a b)")[:, 0:PCOLS].rearrange(
            "p (h n z) -> p h n z", h=2, n=NS)
        onesf = acc[:, 0:128]
        brow = xn2[:, 0:D]

        dense = ctx.enter_context(nc.psum_tensor("dense", [128, 3, 512], F32))
        score = ctx.enter_context(nc.psum_tensor("score", [128, 3, 512], F32))
        pvps = ctx.enter_context(nc.psum_tensor("pvps", [128, 2, 512], F32))

        s_w, s_pix, s_txt = sem("s_w"), sem("s_pix"), sem("s_txt")
        s_qks = [[sem(f"s_qks{u}{i}") for i in range(2)] for u in range(2)]
        s_stack = [sem(f"s_stack{b}") for b in range(2)]
        s_ms = [sem(f"s_ms{b}") for b in range(2)]
        s_mi = [sem(f"s_mi{b}") for b in range(2)]
        s_out = sem("s_out")
        s_apart = sem("s_apart")
        pe = {n: sem("pe_" + n) for n in ["pix", "emb", "ht", "xt", "qk", "v", "s", "st", "pv", "mt",
                                          "ct", "o", "x2t", "up", "ss", "dn", "init"]}
        a = {n: sem("a_" + n) for n in ["ro", "pix", "emb", "xt", "qk0", "qk1", "v0", "v1", "exp", "mt",
                                        "ct", "x2t", "gelu", "sq", "w"]}
        v = {n: sem("v_" + n) for n in ["pix", "h", "st1", "mv1", "xn", "xt", "qkr", "qk2", "vr", "v2",
                                        "max", "m0", "mr", "m1", "m2", "pl", "cu", "ct", "h2", "st2",
                                        "mv2", "xn2", "x2t", "gl", "accl", "ss", "fin", "w"]}
        p = {n: sem("p_" + n) for n in ["mask", "cx", "bo", "rstd1", "ln2", "acc", "ss", "w"]}

        def need(eng, s, per, pair, k):
            if not isinstance(pair, int):
                eng.wait_ge(s, pair * per + k)
            elif pair >= 0:
                eng.wait_ge(s, min(pair, NPAIR - 1) * per + k)

        def apart(eng):
            eng.sem_inc(s_apart, 1)

        released = {"pix": v["pix"], "emb": a["emb"], "ht": v["h"], "xt": v["xt"], "qk": v["qkr"],
                    "v": v["vr"], "ct": v["ct"], "o": v["h2"], "x2t": v["x2t"], "up": a["gelu"],
                    "ss": v["ss"], "dn": v["fin"]}

        def live(pair):
            return not isinstance(pair, int) or 0 <= pair < NPAIR

        def dense_bank(eng, t, name, k):
            n = DENSE.index((name, k))
            m, back = n - 3, 0
            while True:
                if m < 0:
                    m, back = m + NDENSE, back + 1
                if back > 2:
                    break
                other, j = DENSE[m]
                if other != "spare":
                    pair = t - back - LAG[other]
                    if live(pair):
                        eng.wait_ge(released[other], pair * PER[other] + j + 1)
                        break
                m -= 3
            return dense[:, n % 3]

        def bank_of(name, k):
            return dense[:, DENSE.index((name, k)) % 3]

        def hi_view(ap2d):
            return ap2d.bitcast(BF16)[:, 1::2]

        def col(blk, b):
            return b * S + blk * R

        def steps(body, eng):
            for t in range(4):
                body(t, t % 2)
            with eng.Fori(4, NPAIR - 2, 2) as i:
                body(i, 0)
                body(i + 1, 1)
            for t in range(NPAIR - 2, NPAIR + 3):
                body(t, t % 2)

        block = ctx.enter_context(nc.Block())

        @block.sync
        def _(sp):
            for i, (dst, src) in enumerate([
                    (g[:].rearrange("p a b -> p (a b)")[:, 0:1536], w_embed),
                    (g[:].rearrange("p a b -> p (a b)")[:, 1536:3584], wqkvo),
                    (h[:].rearrange("p a b -> p (a b)"), w_upT),
                    (h2[:].rearrange("p a b -> p (a b)"), w_downT),
                    (posb[:], pos), (brow, b_embed), (borow[:], bo)]):
                sp.dma_start(dst, src).then_inc(s_w, 16)
            xp = x.rearrange("b c (n q) w -> (b c n) (q w)", q=PATCH)

            def load_pixels(pair):
                sp.dma_start(pix[:], xp[bass.ds(pair * PROWS, PROWS), :]).then_inc(s_pix, 16)

            load_pixels(0)

            def step(t, u):
                for b in range(2):
                    if live(t - 1):
                        need(sp, pe["st"], 24, t - 2, 12 * b + 12)
                        for i in range(2):
                            need(sp, s_qks[1 - u][i], 32, (t - 1 - (1 - u)) // 2 if isinstance(t, int) else None, 32) \
                                if isinstance(t, int) else sp.wait_ge(s_qks[1 - u][i], (t - 1 + u) * 16 + 16)
                        for which, st in ((0, qst[b]), (1, kst[b])):
                            for j, parts in enumerate(PARTS):
                                src = qk_scr[1 - u, which, :, parts[which], b]
                                sp.dma_start(st[16 * j:16 * j + 16, 0:HS].rearrange("d (m z) -> d m z", m=2),
                                             src.rearrange("m (d e) s -> d m (e s)", d=HD)
                                             ).then_inc(s_stack[b], 16)
                    if b == 0 and live(t + 1) and live(t):
                        if not isinstance(t, int) or t + 1 < NPAIR:
                            need(sp, a["ro"], 2, t, 2)
                            load_pixels(t + 1)
                if live(t):
                    if isinstance(t, int) and t < 2:
                        sp.wait_ge(v["w"], 8)
                    need(sp, v["h2"], 2, t - 2, 2)
                    need(sp, p["bo"], 1, t - 2, 1)
                    sp.dma_start(h[RP1:R, u, 2 * D:4 * D].rearrange("p (b d) -> p b d", b=2),
                                 txt[bass.ds(t * 2, 2)].rearrange("b r d -> r b d")).then_inc(s_txt, 16)

                def maxima(b):
                    if live(t - 1):
                        need(sp, a["mt"], 2, t - 1, b + 1)
                        sp.dma_start(m_scr[1 - u, b], mT[:, b]).then_inc(s_ms[b], 16)
                        sp.wait_ge(s_ms[b], (t - 1) * 16 + 16)
                        sp.dma_start(qst[b][KS:KM, 0:HS],
                                     m_scr[1 - u, b].rearrange("(c e) s -> c (e s)", c=3)).then_inc(s_mi[b], 16)

                def store_parts(k):
                    if live(t):
                        need(sp, v["qk2"], 4, t, k + 1)
                        sp.dma_start(qk_scr[u, k // 2, k % 2].rearrange("c b f s -> f c b s"),
                                     qkp[:, k % 2].rearrange("p c (b s) -> p c b s", b=2)
                                     ).then_inc(s_qks[u][k % 2], 16)

                maxima(0)
                store_parts(0)
                store_parts(1)
                maxima(1)
                store_parts(2)
                store_parts(3)
                for blk in range(2):
                    if live(t - 3):
                        need(sp, v["fin"], 2, t - 3, blk + 1)
                        sp.dma_start(out[bass.ds((t - 3) * 2, 2), blk * R:blk * R + R].rearrange("b r d -> r b d"),
                                     h2[0:R, 1 - u, 2 * D * blk:2 * D * blk + 2 * D].rearrange(
                                         "p (b d) -> p b d", b=2)).then_inc(s_out, 16)

            steps(step, sp)
            sp.wait_ge(s_out, 32 * NPAIR)

        @block.tensor
        def _(eng):
            def mm(*args, **kw):
                return nc.tensor.matmul(*args, **kw)

            def three(ps, stat, mov, start, stop):
                mm(ps, stat[0], mov[0], start=start, stop=False)
                mm(ps, stat[0], mov[1], start=False, stop=False)
                return mm(ps, stat[1], mov[0], start=False, stop=stop)

            eng.wait_ge(v["w"], 3)
            mm(dense[:, 0, 0:2], onesf, tern[:, 0:2], start=True, stop=True).then_inc(pe["init"], 1)
            eng.wait_ge(p["w"], 6)
            eng.wait_ge(v["w"], 12)

            def pixels(t, k):
                ps = dense_bank(eng, t, "pix", k)
                ph, (n0, n1) = k // 3, NXG[k % 3]
                if k % 3 == 0:
                    need(eng, a["ro"], 2, t, ph + 1)
                for i, n in enumerate(range(n0, n1)):
                    last = nc.tensor.transpose(ps[:, i * PROWS:(i + 1) * PROWS],
                                               patches[:, ph, n], ident[0:PROWS, 0:PROWS])
                last.then_inc(pe["pix"], 1)

            def embed(t, m):
                ps = dense_bank(eng, t, "emb", m)
                need(eng, v["pix"], 6, t, 6)
                o = ps[:, 0:TP].rearrange("p (b n) -> p b n", b=2)
                for ph in range(2):
                    for c in range(C):
                        mov = [q[:, ph].rearrange("p (b c n) -> p b c n", b=2, c=C)[:, :, c] for q in pT]
                        stat = [w[:, 2 * c + ph, m * 128:m * 128 + 128] for w in we]
                        last = three(o, stat, mov, ph == 0 and c == 0, ph == 1 and c == 2)
                last.then_inc(pe["emb"], 1)

            def hidden_rows(t, blk):
                ps = dense_bank(eng, t, "ht", blk)
                if blk == 0:
                    need(eng, a["emb"], 2, t, 2)
                w = R if blk == 0 else RP1
                for b in range(2):
                    for m in range(2):
                        c0 = b * NPATCH + blk * R
                        last = nc.tensor.transpose(ps[0:w, b * D + m * 128:b * D + m * 128 + 128],
                                                   hT[:, m, c0:c0 + w], ident[:])
                last.then_inc(pe["ht"], 1)

            def to_columns(t, name, m, src):
                ps = dense_bank(eng, t, name, m)
                for blk in range(2):
                    for b in range(2):
                        c0 = (2 * blk + b) * D + m * 128
                        last = nc.tensor.transpose(ps[:, col(blk, b):col(blk, b) + R], src[:, c0:c0 + 128],
                                                   ident[0:R, 0:R])
                last.then_inc(pe[name], 1)

            def queries_keys(t, k):
                ps = dense_bank(eng, t, "qk", k)
                if k == 0:
                    need(eng, v["xt"], 2, t, 2)
                for c in range(2):
                    last = three(ps[:, 0:T2], [w[:, k // 2, c, (k % 2) * 128:(k % 2) * 128 + 128] for w in wa],
                                 [q[:, c] for q in aT], c == 0, c == 1)
                last.then_inc(pe["qk"], 1)

            def token_product(t, name, blk, wi):
                ps = dense_bank(eng, t, name, blk)
                for b in range(2):
                    for c in range(2):
                        last = three(ps[0:R, b * D:b * D + D],
                                     [q[:, c, col(blk, b):col(blk, b) + R] for q in aT],
                                     [w[:, wi, c] for w in wa], c == 0, c == 1)
                last.then_inc(pe[name], 1)

            def up(t, m):
                ps = dense_bank(eng, t, "up", m)
                if m == 0:
                    need(eng, v["x2t"], 2, t - 3, 2)
                for c in range(2):
                    for i in range(2):
                        last = mm(ps[:, 0:T2], wup[:, c, m * 128:m * 128 + 128], xT2[i][:, c],
                                  start=(c == 0 and i == 0), stop=(c == 1 and i == 1))
                last.then_inc(pe["up"], 1)

            def sum_squares(t):
                ps = dense_bank(eng, t, "ss", 0)
                need(eng, v["accl"], 1, t - 3, 1)
                for j in range(4):
                    c0 = col(j // 2, j % 2)
                    mm(ps[0:R, j:j + 1], hi_view(acc[:, c0:c0 + R]), onesb[:, 0:1], start=True, stop=False)
                    last = mm(ps[0:R, j:j + 1], accl[:, c0:c0 + R], onesb[:, 0:1], start=False, stop=True)
                last.then_inc(pe["ss"], 1)

            def down(t, blk):
                ps = dense_bank(eng, t, "dn", blk)
                if blk == 0:
                    need(eng, v["gl"], 8, t - 3, 8)
                for b in range(2):
                    c0 = col(blk, b)
                    for m in range(NFF):
                        mm(ps[0:R, b * D:b * D + D], hi_view(g[:, m, c0:c0 + R]), wdn[:, m],
                           start=(m == 0), stop=False)
                        last = mm(ps[0:R, b * D:b * D + D], gl[:, m, c0:c0 + R], wdn[:, m],
                                  start=False, stop=(m == NFF - 1))
                last.then_inc(pe["dn"], 1)

            def heads_of(n):
                g4, k = divmod(n, 3)
                return (range(4 * g4, 4 * g4 + 4), False) if k == 2 else (range(4 * g4 + 2 * k, 4 * g4 + 2 * k + 2), True)

            def scores_columns(t, n):
                b, k = divmod(n, 12)
                if k == 0:
                    need(eng, s_mi[b], 16, t - 2, 16)
                if n >= 3:
                    need(eng, a["exp"], 24, t - 2, n - 2)
                elif live(t - 2) and not (isinstance(t, int) and t < 2):
                    need(eng, v["max"], 24, t - 2, 24 - 2 + n)
                heads, both = heads_of(k)
                for i, hd in enumerate(heads):
                    c0 = hd * S + (0 if both else R)
                    w = S if both else R
                    last = mm(score[:, n % 3, i * w:i * w + w], kst[b][0:KM, c0:c0 + 128],
                              qst[b][0:KM, c0:c0 + w], start=True, stop=True)
                last.then_inc(pe["st"], 1)

            def scores_rows(t, n):
                b, k = divmod(n, 12)
                if k == 0:
                    need(eng, s_stack[b], 192, t - 1, 192)
                if n >= 3:
                    need(eng, v["max"], 24, t - 1, n - 2)
                elif live(t - 2):
                    need(eng, a["exp"], 24, t - 2, 24 - 2 + n)
                heads, both = heads_of(k)
                w = S if both else R
                for i, hd in enumerate(heads):
                    c0 = hd * S + (R if both else 0)
                    mm(score[:, n % 3, i * w:i * w + w], qst[b][0:KS, c0:c0 + 128],
                       kst[b][0:KS, hd * S:hd * S + w], start=(i == 0), stop=False, skip_group_check=True)
                nh = len(heads)
                o = score[:, n % 3, 0:T2].rearrange("p (i w) -> p i w", i=nh)[:, :, w - R:w]
                last = mm(o, identb[0:R, :], cmask[0:R].rearrange("p (o w) -> p o w", o=1).broadcast_to([R, nh, R]),
                          start=False, stop=True, skip_group_check=True)
                last.then_inc(pe["s"], 1)

            def weighted_values(t, u, gi):
                b, g4 = divmod(gi, 4)
                need(eng, v["pl"], 8, t - 2, gi + 1)
                if gi == 0:
                    need(eng, v["v2"], 2, t - 2, 2)
                if gi >= 2:
                    need(eng, v["cu"], 8, t - 2, gi - 1)
                elif not (isinstance(t, int) and t < 3):
                    need(eng, a["mt"], 2, t - 2, gi + 1)
                else:
                    need(eng, a["mt"], 2, t - 2, gi + 1)
                P_, L_ = pr[gi % 2], pl[gi % 2]
                for qb in range(2):
                    for i in range(4):
                        hd = 4 * g4 + i
                        o = pvps[:, gi % 2, (4 * qb + i) * VW:(4 * qb + i) * VW + VW]
                        for kb in range(qb + 1):
                            c0 = i * S + qb * R if kb == 0 else 2 * T2 + i * R
                            val = vp[:, u, 2 * kb + b, hd]
                            mm(o, hi_view(P_[:, c0:c0 + 128]), val, start=(kb == 0), stop=False)
                            last = mm(o[:, 0:1 + 2 * HD], L_[:, c0:c0 + 128], val[:, 0:1 + 2 * HD],
                                      start=False, stop=(kb == qb))
                last.then_inc(pe["pv"], 1)

            def maxima_rows(t, b):
                need(eng, v["m2"], 2, t - 1, b + 1)
                if live(t - 2):
                    need(eng, v["cu"], 8, t - 2, 7 + b)
                apart(eng)
                for qb in range(2):
                    last = nc.tensor.transpose(pvps[0:48, b, 0:256].bitcast(BF16)[:, qb * R:qb * R + R],
                                               mp[:, b, qb].rearrange("p c e -> p (c e)"), identb[0:R, 0:R])
                last.then_inc(pe["mt"], 1)

            def step(t, u):
                A, Bm, Cc, Dd = live(t), live(t - 1), live(t - 2), live(t - 3)
                for gi in range(9):
                    if Cc and gi < 8:
                        for n in range(3):
                            scores_columns(t, 3 * gi + n)
                    if A and 1 <= gi < 4:
                        pixels(t, 2 * gi - 2)
                        pixels(t, 2 * gi - 1)
                    if A and gi in (4, 6):
                        embed(t, (gi - 4) // 2)
                    if Cc and gi >= 1:
                        weighted_values(t, u, gi - 1)
                if Cc:
                    need(eng, p["cx"], 8, t - 2, 8)
                    to_columns(t, "ct", 0, cx[:].rearrange("p j d -> p (j d)"))
                    to_columns(t, "ct", 1, cx[:].rearrange("p j d -> p (j d)"))
                if Dd:
                    up(t, 0)
                    up(t, 1)
                if Cc:
                    need(eng, v["ct"], 2, t - 2, 2)
                    token_product(t, "o", 0, 3)
                    token_product(t, "o", 1, 3)
                if A:
                    hidden_rows(t, 0)
                    hidden_rows(t, 1)
                for k in range(4):
                    if Bm:
                        for n in range(6):
                            scores_rows(t, 6 * k + n)
                        if k == 2:
                            maxima_rows(t, 0)
                    if Dd and k < 3:
                        up(t, 2 + k)
                    if k == 2:
                        if Dd:
                            up(t, 5)
                        if A:
                            need(eng, v["xn"], 4, t, 4)
                            to_columns(t, "xt", 0, xn)
                            to_columns(t, "xt", 1, xn)
                if Dd:
                    up(t, 6)
                    up(t, 7)
                if A:
                    queries_keys(t, 0)
                    queries_keys(t, 1)
                if Bm:
                    maxima_rows(t, 1)
                if A:
                    queries_keys(t, 2)
                    queries_keys(t, 3)
                    token_product(t, "v", 0, 2)
                    token_product(t, "v", 1, 2)
                if Dd:
                    sum_squares(t)
                    down(t, 0)
                    down(t, 1)
                if Cc:
                    need(eng, v["xn2"], 4, t - 2, 4)
                    to_columns(t, "x2t", 0, xn2[:])
                    to_columns(t, "x2t", 1, xn2[:])

            steps(step, eng)

        @block.scalar
        def _(eng):
            act = nc.scalar.activation
            gf = g[:].rearrange("p a b -> p (a b)")
            eng.wait_ge(s_w, 16 * 7)
            act(we[0][:].rearrange("p a b -> p (a b)"), gf[:, 0:1536], ACT.Copy).then_inc(a["w"], 1)
            act(wa[0][:].rearrange("p a b c -> p (a b c)"), gf[:, 1536:3584], ACT.Copy).then_inc(a["w"], 1)

            def reorder(t, ph):
                if ph == 0:
                    need(eng, s_pix, 16, t, 16)
                    need(eng, pe["dn"], 2, t - 4, 2)
                    if isinstance(t, int) and t == 0:
                        eng.wait_ge(v["w"], 11)
                half = PCOLS // 2
                act(patches[:, ph].rearrange("p n (q w) -> p q n w", q=8),
                    pix[:, ph * half:ph * half + half].rearrange("p (q n w) -> p q n w", q=8, n=NS),
                    ACT.Copy).then_inc(a["ro"], 1)

            def pixels_hi(t, k):
                n0, n1 = NXG[k % 3]
                need(eng, pe["pix"], 6, t, k + 1)
                if k == 0:
                    need(eng, pe["emb"], 2, t - 1, 2)
                src = bank_of("pix", k)[:, 0:(n1 - n0) * PROWS].rearrange("p (n r) -> p r n", r=PROWS)
                dst = pT[0][:, k // 3].rearrange("p (r n) -> p r n", n=NS)[:, :, n0:n1]
                act(dst, src, ACT.Copy).then_inc(a["pix"], 1)

            def hi_part(t, name, m, dst, pair):
                need(eng, pe[name], 2, pair, m + 1)
                act(dst[:, m], bank_of(name, m)[:, 0:T2], ACT.Copy).then_inc(a[name], 1)

            def exponentials(t, gi):
                Pb = pr[gi % 2]
                for k in range(3):
                    n = 3 * gi + k
                    need(eng, pe["st"], 24, t - 2, n + 1)
                    if k == 0 and gi >= 2:
                        need(eng, pe["pv"], 8, t - 2, gi - 1)
                    elif k == 0:
                        need(eng, pe["pv"], 8, t - 3, 7 + gi)
                    act(Pb[:, k * T2:k * T2 + T2], score[0:R, n % 3, 0:T2], ACT.Exp,
                        scale=float(HD) ** -0.5).then_inc(a["exp"], 1)

            def gelu(t, m):
                need(eng, pe["up"], 8, t - 3, m + 1)
                if m == 0:
                    need(eng, pe["dn"], 2, t - 4, 2)
                    need(eng, pe["pix"], 6, t, 6)
                act(g[:, m], bank_of("up", m)[:, 0:T2], ACT.Gelu).then_inc(a["gelu"], 1)
                need(eng, a["gelu"], 8, t - 3, m + 1)
                if m >= 2:
                    need(eng, p["acc"], 7, t - 3, max(1, m - 2))
                else:
                    need(eng, p["acc"], 7, t - 4, 7)
                act(sq[:, m % 2], g[:, m], ACT.Square).then_inc(a["sq"], 1)

            def part_qk(t, k):
                need(eng, pe["qk"], 4, t, k + 1)
                if k >= 2:
                    stored(t, k % 2, 1)
                else:
                    stored(t - 1, k % 2, 2)
                act(qkp[:, k % 2, 0], bank_of("qk", k)[:, 0:T2], ACT.Copy).then_inc(a["qk0"], 1)
                need(eng, v["qkr"], 4, t, k + 1)
                act(qkp[:, k % 2, 1], qkr[:], ACT.Copy).then_inc(a["qk1"], 1)

            def stored(pair, i, times):
                if isinstance(pair, int):
                    if pair >= 0:
                        eng.wait_ge(s_qks[pair % 2][i], (pair // 2) * 32 + 16 * times)
                else:
                    uu = parity[0] if times == 1 else 1 - parity[0]
                    eng.wait_ge(s_qks[uu][i], (pair - uu) * 16 + 16 * times)

            def part_v(t, u, blk):
                need(eng, pe["v"], 2, t, blk + 1)
                if blk == 0:
                    need(eng, pe["pv"], 8, t - 2, 8)
                dst = [vp[:, u, 2 * blk:2 * blk + 2].rearrange("p b e c -> p (b e) c")[:, :, 1 + HD * i:1 + HD * i + HD]
                       for i in range(3)]
                act(dst[0], bank_of("v", blk)[0:R, 0:2 * D].rearrange("p (e c) -> p e c", c=HD),
                    ACT.Copy).then_inc(a["v0"], 1)
                need(eng, v["vr"], 2, t, blk + 1)
                act(dst[1], vr[:].rearrange("p (e c) -> p e c", c=HD), ACT.Copy).then_inc(a["v1"], 1)

            def maxima(t, b):
                need(eng, pe["mt"], 2, t - 1, b + 1)
                need(eng, s_ms[b], 16, t - 2, 16)
                act(mT[:, b], pvps[0:48, b, 0:256].bitcast(BF16)[:, 0:S], ACT.Copy).then_inc(a["mt"], 1)

            parity = [0]

            def step(t, u):
                parity[0] = u
                A, Bm, Cc, Dd = live(t), live(t - 1), live(t - 2), live(t - 3)
                for gi in range(8):
                    if A and gi < 2:
                        reorder(t, gi)
                    if Cc:
                        exponentials(t, gi)
                    if A and 1 <= gi < 4:
                        pixels_hi(t, 2 * gi - 2)
                        pixels_hi(t, 2 * gi - 1)
                    if A and gi in (5, 7):
                        m = (gi - 5) // 2
                        need(eng, pe["emb"], 2, t, m + 1)
                        if m == 0:
                            need(eng, pe["ht"], 2, t - 1, 2)
                        act(hT[:, m], bank_of("emb", m)[:, 0:TP], ACT.Copy).then_inc(a["emb"], 1)
                if Cc:
                    need(eng, pe["v"], 2, t - 1, 2)
                    hi_part(t, "ct", 0, aT[0], t - 2)
                    hi_part(t, "ct", 1, aT[0], t - 2)
                if Dd:
                    gelu(t, 0)
                    gelu(t, 1)
                for k in range(3):
                    if Dd:
                        gelu(t, 2 + k)
                if Bm:
                    maxima(t, 0)
                if Dd:
                    gelu(t, 5)
                if A:
                    need(eng, pe["o"], 2, t - 2, 2)
                    hi_part(t, "xt", 0, aT[0], t)
                    hi_part(t, "xt", 1, aT[0], t)
                if Dd:
                    gelu(t, 6)
                    gelu(t, 7)
                if A:
                    part_qk(t, 0)
                    part_qk(t, 1)
                if Bm:
                    maxima(t, 1)
                if A:
                    part_qk(t, 2)
                    part_qk(t, 3)
                    part_v(t, u, 0)
                    part_v(t, u, 1)
                if Cc:
                    need(eng, pe["up"], 8, t - 3, 8)
                    hi_part(t, "x2t", 0, xT2[0], t - 2)
                    hi_part(t, "x2t", 1, xT2[0], t - 2)

            steps(step, eng)

        @block.vector
        def _(eng):
            tt, ts = nc.vector.tensor_tensor, nc.vector.tensor_scalar
            gf = g[:].rearrange("p a b -> p (a b)")
            hf, h2f = h[:].rearrange("p a b -> p (a b)"), h2[:].rearrange("p a b -> p (a b)")
            eng.memset(onesb[:], 1.0)
            for i, e in enumerate((-0.5, 0.5, -1.0)):
                eng.memset(exps[:, i], e)
            for b in range(2):
                eng.memset(qst[b][:, HS:], 0.0)
                eng.memset(kst[b][:, HS:], 0.0)
                eng.memset(kst[b][KS:KM, 0:HS], 1.0)
                eng.memset(pr[b][:, 3 * T2:], 0.0)
                eng.memset(pl[b][:, 3 * T2:], 0.0)
            eng.memset(vp[:, :, :, :, 0:1].rearrange("p u j e c -> p (u j e) c"), 1.0)
            eng.memset(onesf, 1.0).then_inc(v["w"], 1)
            eng.wait_ge(s_w, 16 * 7)
            nc.vector.tensor_reduce(tern[:, 0:1], hf, AX.X, ALU.add, apply_absolute_value=True).then_inc(v["w"], 1)
            nc.vector.tensor_reduce(tern[:, 1:2], h2f, AX.X, ALU.add, apply_absolute_value=True).then_inc(v["w"], 1)
            eng.wait_ge(pe["init"], 1)
            ts(tern[:, 2:4], dense[:, 0, 0:2], 0.5 / (D * FF), None, ALU.mult).then_inc(v["w"], 1)
            ts(tern[:, 4:6], dense[:, 0, 0:2], -0.5 / (D * FF), None, ALU.mult).then_inc(v["w"], 1)
            eng.wait_ge(v["w"], 5)
            for i, (src, dst) in enumerate(((hf, wup[:].rearrange("p a b -> p (a b)")),
                                            (h2f, wdn[:].rearrange("p a b -> p (a b)")))):
                below = pT[0][:].bitcast(F32).rearrange("p a b -> p (a b)")[:, 0:2048] if False else gf[:, 0:2048]
                if i == 0:
                    eng.wait_ge(a["w"], 2)
                    tt(we[1][:].rearrange("p a b -> p (a b)"), gf[:, 0:1536],
                       we[0][:].bitcast(F32).rearrange("p a b -> p (a b)"), ALU.subtract).then_inc(v["w"], 1)
                    tt(wa[1][:].rearrange("p a b c -> p (a b c)"), gf[:, 1536:3584],
                       wa[0][:].bitcast(F32).rearrange("p a b c -> p (a b c)"), ALU.subtract).then_inc(v["w"], 1)
                    eng.wait_ge(v["w"], 7)
                else:
                    eng.wait_ge(v["w"], 9)
                ts(below, src, tern[:, 4 + i:5 + i], None, ALU.is_lt).then_inc(v["w"], 1)
                if i == 0:
                    eng.wait_ge(v["w"], 8)
                else:
                    eng.wait_ge(v["w"], 10)
                nc.vector.scalar_tensor_tensor(out=dst, in0=src, scalar=tern[:, 2 + i:3 + i], in1=below,
                                               op0=ALU.is_gt, op1=ALU.subtract).then_inc(v["w"], 1)
            tt(posb[:], posb[:], brow.rearrange("p (o d) -> p o d", o=1).broadcast_to([R, 2, D]),
               ALU.add).then_inc(v["w"], 1)
            eng.wait_ge(v["w"], 12)

            def pixels_lo(t, k):
                n0, n1 = NXG[k % 3]
                need(eng, a["pix"], 6, t, k + 1)
                src = bank_of("pix", k)[:, 0:(n1 - n0) * PROWS].rearrange("p (n r) -> p r n", r=PROWS)
                hi, lo = [q[:, k // 3].rearrange("p (r n) -> p r n", n=NS)[:, :, n0:n1] for q in
                          (pT[0][:].bitcast(F32), pT[1])]
                tt(lo, src, hi, ALU.subtract).then_inc(v["pix"], 1)

            def lo_part(name, m, hi, lo, pair):
                need(eng, a[name], 2, pair, m + 1)
                tt(lo[:, m], bank_of(name, m)[:, 0:T2], hi[:, m], ALU.subtract).then_inc(v[name], 1)

            def remainders(t, gi):
                need(eng, p["mask"], 16, t - 2, 2 * gi + 2)
                if gi >= 2:
                    need(eng, pe["pv"], 8, t - 2, gi - 1)
                else:
                    need(eng, pe["pv"], 8, t - 3, 7 + gi)
                Pb = pr[gi % 2][:, 0:3 * T2]
                tt(pl[gi % 2][:, 0:3 * T2], Pb, hi_view(Pb), ALU.subtract).then_inc(v["pl"], 1)

            def collect(t, gi):
                need(eng, pe["pv"], 8, t - 2, gi + 1)
                if gi >= 2:
                    need(eng, p["cx"], 8, t - 2, gi - 1)
                else:
                    need(eng, p["cx"], 8, t - 3, 7 + gi)
                bank = pvps[0:R, gi % 2, 0:8 * VW].rearrange("p (e c) -> p e c", c=VW)
                nc.vector.reciprocal(rs[:, gi % 2], bank[:, :, 0:1].rearrange("p e c -> p (e c)"))
                nc.vector.tensor_reduce(cu[:, gi % 2], bank[:, :, 1:VW].rearrange("p e (k d) -> p e d k", k=3),
                                        AX.X, ALU.add).then_inc(v["cu"], 1)

            def gelu_lo(t, m):
                need(eng, a["gelu"], 8, t - 3, m + 1)
                if m == 0:
                    need(eng, pe["dn"], 2, t - 4, 2)
                tt(gl[:, m], g[:, m], hi_view(g[:, m]), ALU.subtract).then_inc(v["gl"], 1)

            def residual(t, u, blk):
                need(eng, pe["o"], 2, t - 2, blk + 1)
                if blk == 0:
                    need(eng, s_out, 32, t - 4, 32)
                    need(eng, p["bo"], 1, t - 2, 1)
                w = slice(2 * D * blk, 2 * D * blk + 2 * D)
                tt(h2[0:R, u, w], bank_of("o", blk)[0:R, 0:2 * D], h[0:R, u, w], ALU.add).then_inc(v["h2"], 1)

            def moments(t, src, st, mv, s_st, s_mv, pair, free, name):
                for j in range(4):
                    eng.bn_stats(st[:, j], src[:, j * D:j * D + D]).then_inc(s_st, 1)
                need(eng, s_st, 4, pair, 4)
                apart(eng)
                for j in range(4):
                    eng.bn_aggr(mv[:, j], st[:, j]).then_inc(s_mv, 1)

            def maxima_unit(t, n):
                b, k = divmod(n, 12)
                g4, j = divmod(k, 3)
                need(eng, pe["s"], 24, t - 1, n + 1)
                qb, h0, nh = (0, 4 * g4, 4) if j == 2 else (1, 4 * g4 + 2 * j, 2)
                if n == 0:
                    need(eng, v["m2"], 2, t - 2, 2)
                nc.vector.tensor_reduce(mx[:, b, qb, h0:h0 + nh],
                                        score[0:R, n % 3, 0:T2].rearrange("p (i w) -> p i w", i=nh),
                                        AX.X, ALU.max).then_inc(v["max"], 1)

            def maxima_parts(t, b):
                need(eng, v["max"], 24, t - 1, 12 * b + 12)
                need(eng, pe["mt"], 2, t - 2, b + 1)
                part = [mp[:, b, :, i] for i in range(3)]
                ts(part[0], mx[:, b], -1.0, None, ALU.mult).then_inc(v["m0"], 1)
                need(eng, v["m0"], 2, t - 1, b + 1)
                nc.vector.scalar_tensor_tensor(out=mr[:, b], in0=mx[:, b], scalar=-1.0, in1=part[0],
                                               op0=ALU.mult, op1=ALU.subtract).then_inc(v["mr"], 1)
                need(eng, v["mr"], 2, t - 1, b + 1)
                nc.vector.tensor_copy(part[1], mr[:, b]).then_inc(v["m1"], 1)
                need(eng, v["m1"], 2, t - 1, b + 1)
                tt(part[2], mr[:, b], part[1], ALU.subtract).then_inc(v["m2"], 1)

            def hidden(t, u, blk):
                need(eng, pe["ht"], 2, t, blk + 1)
                if blk == 0:
                    need(eng, v["h2"], 2, t - 2, 2)
                w = R if blk == 0 else RP1
                tt(h[0:w, u, 2 * D * blk:2 * D * blk + 2 * D].rearrange("p (b d) -> p b d", b=2),
                   bank_of("ht", blk)[0:w].rearrange("p (b d) -> p b d", b=2),
                   posb[0:w, blk].rearrange("p (o d) -> p o d", o=1).broadcast_to([w, 2, D]),
                   ALU.add).then_inc(v["h"], 1)

            def qk_rest(t, k):
                need(eng, a["qk0"], 4, t, k + 1)
                need(eng, v["qk2"], 4, *((t, k) if k else (t - 1, 4)))
                tt(qkr[:], bank_of("qk", k)[:, 0:T2], qkp[:, k % 2, 0], ALU.subtract).then_inc(v["qkr"], 1)
                need(eng, a["qk1"], 4, t, k + 1)
                tt(qkp[:, k % 2, 2], qkr[:], qkp[:, k % 2, 1], ALU.subtract).then_inc(v["qk2"], 1)

            def v_rest(t, u, blk):
                dst = [vp[:, u, 2 * blk:2 * blk + 2].rearrange("p b e c -> p (b e) c")[:, :, 1 + HD * i:1 + HD * i + HD]
                       for i in range(3)]
                r3 = vr[:].rearrange("p (e c) -> p e c", c=HD)
                need(eng, a["v0"], 2, t, blk + 1)
                need(eng, v["v2"], 2, *((t, blk) if blk else (t - 1, 2)))
                tt(r3, bank_of("v", blk)[0:R, 0:2 * D].rearrange("p (e c) -> p e c", c=HD), dst[0],
                   ALU.subtract).then_inc(v["vr"], 1)
                need(eng, a["v1"], 2, t, blk + 1)
                tt(dst[2], r3, dst[1], ALU.subtract).then_inc(v["v2"], 1)

            def final(t, blk, u):
                need(eng, pe["dn"], 2, t - 3, blk + 1)
                if blk == 0:
                    need(eng, p["ss"], 3, t - 3, 3)
                for b in range(2):
                    w = slice((2 * blk + b) * D, (2 * blk + b + 1) * D)
                    last = nc.vector.scalar_tensor_tensor(
                        out=h2[0:R, 1 - u, w], in0=bank_of("dn", blk)[0:R, b * D:b * D + D],
                        scalar=ssq[:, 2, 2 * blk + b:2 * blk + b + 1], in1=h2[0:R, 1 - u, w],
                        op0=ALU.mult, op1=ALU.add)
                last.then_inc(v["fin"], 1)

            def step(t, u):
                A, Bm, Cc, Dd = live(t), live(t - 1), live(t - 2), live(t - 3)
                for gi in range(9):
                    if A and 1 <= gi < 4:
                        pixels_lo(t, 2 * gi - 2)
                        pixels_lo(t, 2 * gi - 1)
                    if Cc and gi < 8:
                        remainders(t, gi)
                    if Cc and gi >= 1:
                        collect(t, gi - 1)
                if Cc:
                    lo_part("ct", 0, aT[0][:].bitcast(F32), aT[1], t - 2)
                    lo_part("ct", 1, aT[0][:].bitcast(F32), aT[1], t - 2)
                if Dd:
                    gelu_lo(t, 0)
                    gelu_lo(t, 1)
                if Cc:
                    residual(t, u, 0)
                    residual(t, u, 1)
                if A:
                    hidden(t, u, 0)
                    hidden(t, u, 1)
                if Cc:
                    need(eng, v["h2"], 2, t - 2, 2)
                    need(eng, v["xn2"], 4, t - 3, 4)
                    need(eng, p["ln2"], 7, t - 3, 7)
                    moments(t, h2[0:R, u], st2, mv2, v["st2"], v["mv2"], t - 2, None, "ln2")
                if A:
                    need(eng, v["h"], 2, t, 2)
                    need(eng, s_txt, 16, t, 16)
                    need(eng, v["xn"], 4, t - 1, 4)
                    need(eng, p["rstd1"], 2, t - 1, 2)
                    moments(t, h[0:R, u], st1, mv1, v["st1"], v["mv1"], t, None, "ln1")
                for k in range(4):
                    if Bm:
                        for n in range(6):
                            maxima_unit(t, 6 * k + n)
                        if k == 1:
                            maxima_parts(t, 0)
                        if k == 3:
                            maxima_parts(t, 1)
                    if Dd and k < 3:
                        gelu_lo(t, 2 + k)
                    if A and k == 0:
                        need(eng, p["rstd1"], 2, t, 2)
                        need(eng, pe["xt"], 2, t - 1, 2)
                        need(eng, pe["ct"], 2, t - 2, 2)
                        for j in range(4):
                            ts(xn[:, j * D:j * D + D], h[0:R, u, j * D:j * D + D], mv1[:, j, 0:1],
                               rstd1[:, 1, j:j + 1], ALU.subtract, ALU.mult).then_inc(v["xn"], 1)
                    if Cc and k == 1:
                        need(eng, p["ln2"], 7, t - 2, 7)
                        need(eng, pe["x2t"], 2, t - 3, 2)
                        for j in range(4):
                            ts(xn2[:, j * D:j * D + D], h2[0:R, u, j * D:j * D + D], mv2[:, j, 0:1],
                               ln2[:, 4, j:j + 1], ALU.subtract, ALU.mult).then_inc(v["xn2"], 1)
                    if k == 2:
                        if Dd:
                            gelu_lo(t, 5)
                        if A:
                            lo_part("xt", 0, aT[0][:].bitcast(F32), aT[1], t)
                            lo_part("xt", 1, aT[0][:].bitcast(F32), aT[1], t)
                if Dd:
                    gelu_lo(t, 6)
                    gelu_lo(t, 7)
                if A:
                    for k in range(4):
                        qk_rest(t, k)
                    v_rest(t, u, 0)
                    v_rest(t, u, 1)
                if Dd:
                    need(eng, p["acc"], 7, t - 3, 7)
                    need(eng, pe["ss"], 1, t - 4, 1)
                    tt(accl[:], acc[:], hi_view(acc[:]), ALU.subtract).then_inc(v["accl"], 1)
                    need(eng, pe["ss"], 1, t - 3, 1)
                    need(eng, p["ss"], 3, t - 4, 3)
                    ts(ssq[:, 0], bank_of("ss", 0)[0:R, 0:4], 1.0 / FF, None, ALU.mult).then_inc(v["ss"], 1)
                    final(t, 0, u)
                    final(t, 1, u)
                if Cc:
                    lo_part("x2t", 0, xT2[0], xT2[1], t - 2)
                    lo_part("x2t", 1, xT2[0], xT2[1], t - 2)

            steps(step, eng)

        @block.gpsimd
        def _(eng):
            tt, ts = nc.gpsimd.tensor_tensor, nc.gpsimd.tensor_scalar
            for idn in (ident, identb):
                eng.memset(idn[:], 0.0).then_inc(p["w"], 1)
            eng.memset(cmask[:], 0.0).then_inc(p["w"], 1)
            eng.wait_ge(p["w"], 3)
            for idn in (ident, identb):
                nc.gpsimd.affine_select(out=idn[:], in_=idn[:], compare_op=ALU.not_equal, fill=1.0, base=0,
                                        pattern=[[-1, 128]], channel_multiplier=1).then_inc(p["w"], 1)
            nc.gpsimd.affine_select(out=cmask[:], in_=cmask[:], compare_op=ALU.is_ge, fill=NEG, base=0,
                                    pattern=[[-1, R]], channel_multiplier=1).then_inc(p["w"], 1)
            eng.wait_ge(v["w"], 1)

            def causal(t, gi):
                need(eng, a["exp"], 24, t - 2, 3 * gi + 3)
                apart(eng)
                Pb = pr[gi % 2]
                both = Pb[:, 0:2 * T2].rearrange("p (e w) -> p e w", e=4)[:, :, 0:R]
                one = Pb[:, 2 * T2:3 * T2].rearrange("p (e w) -> p e w", e=4)
                for blkv in (both, one):
                    nc.gpsimd.affine_select(out=blkv, in_=blkv, compare_op=ALU.is_ge, fill=0.0, base=0,
                                            pattern=[[0, 4], [1, R]], channel_multiplier=-1).then_inc(p["mask"], 1)

            def normalize(t, gi):
                b, g4 = divmod(gi, 4)
                need(eng, v["cu"], 8, t - 2, gi + 1)
                if gi == 0:
                    need(eng, pe["ct"], 2, t - 3, 2)
                    need(eng, pe["xt"], 2, t - 1, 2)
                dst = cx[:].rearrange("p (q b) d -> p q b d", q=2)[:, :, b, 4 * g4 * HD:4 * g4 * HD + 4 * HD]
                tt(dst.rearrange("p q (e d) -> p q e d", e=4), cu[:, gi % 2].rearrange("p (q e) d -> p q e d", q=2),
                   rs[:, gi % 2].rearrange("p (q e o) -> p q e o", q=2, o=1).broadcast_to([R, 2, 4, HD]),
                   ALU.mult).then_inc(p["cx"], 1)

            def accumulate(t, m):
                need(eng, a["sq"], 8, t - 3, m + 1)
                if m == 1:
                    need(eng, pe["ss"], 1, t - 4, 1)
                    need(eng, v["accl"], 1, t - 4, 1)
                else:
                    need(eng, p["acc"], 7, t - 3, m - 1)
                tt(acc[:], sq[:, 0] if m == 1 else acc[:], sq[:, m % 2], ALU.add).then_inc(p["acc"], 1)

            def step(t, u):
                A, Bm, Cc, Dd = live(t), live(t - 1), live(t - 2), live(t - 3)
                for gi in range(9):
                    if Cc and gi < 8:
                        causal(t, gi)
                    if Cc and gi >= 1:
                        normalize(t, gi - 1)
                if Dd:
                    accumulate(t, 1)
                if Cc:
                    need(eng, v["mv2"], 4, t - 2, 4)
                    need(eng, v["xn2"], 4, t - 3, 4)
                    apart(eng)
                    var = mv2[:, :, 1:2].rearrange("p j o -> p (j o)")
                    ts(ln2[:, 5], var, EPS, None, ALU.add).then_inc(p["ln2"], 1)
                    tt(ln2[:, 1], var, exps[:, 1], ALU.pow).then_inc(p["ln2"], 1)
                    need(eng, p["ln2"], 7, t - 2, 2)
                    tt(ln2[:, 0], ln2[:, 5], exps[:, 0], ALU.pow).then_inc(p["ln2"], 1)
                    need(eng, p["ln2"], 7, t - 2, 3)
                    tt(ln2[:, 2], ln2[:, 0], ln2[:, 1], ALU.mult).then_inc(p["ln2"], 1)
                    need(eng, p["ln2"], 7, t - 2, 4)
                    apart(eng)
                    ts(ln2[:, 3], ln2[:, 2], RMS_EPS, None, ALU.add).then_inc(p["ln2"], 1)
                    need(eng, p["ln2"], 7, t - 2, 5)
                    tt(ln2[:, 6], ln2[:, 3], exps[:, 2], ALU.pow).then_inc(p["ln2"], 1)
                    need(eng, p["ln2"], 7, t - 2, 6)
                    tt(ln2[:, 4], ln2[:, 0], ln2[:, 6], ALU.mult).then_inc(p["ln2"], 1)
                if A:
                    need(eng, v["mv1"], 4, t, 4)
                    need(eng, v["xn"], 4, t - 1, 4)
                    apart(eng)
                    ts(rstd1[:, 0], mv1[:, :, 1:2].rearrange("p j o -> p (j o)"), EPS, None,
                       ALU.add).then_inc(p["rstd1"], 1)
                    need(eng, p["rstd1"], 2, t, 1)
                    tt(rstd1[:, 1], rstd1[:, 0], exps[:, 0], ALU.pow).then_inc(p["rstd1"], 1)
                if Dd:
                    accumulate(t, 2)
                    accumulate(t, 3)
                if A:
                    need(eng, v["xn"], 4, t, 4)
                    hb = h[0:R, u].rearrange("p (j d) -> p j d", j=4)
                    tt(hb, hb, borow[:].rearrange("p (o d) -> p o d", o=1).broadcast_to([R, 4, D]),
                       ALU.add).then_inc(p["bo"], 1)
                if Dd:
                    for m in range(4, 8):
                        accumulate(t, m)
                    need(eng, v["ss"], 1, t - 3, 1)
                    need(eng, v["fin"], 2, t - 4, 2)
                    tt(ssq[:, 1], ssq[:, 0], exps[:, 1], ALU.pow).then_inc(p["ss"], 1)
                    need(eng, p["ss"], 3, t - 3, 1)
                    apart(eng)
                    ts(ssq[:, 3], ssq[:, 1], RMS_EPS, None, ALU.add).then_inc(p["ss"], 1)
                    need(eng, p["ss"], 3, t - 3, 2)
                    tt(ssq[:, 2], ssq[:, 3], exps[:, 2], ALU.pow).then_inc(p["ss"], 1)

            steps(step, eng)


def kernel(x, txt, L0_tok_W_embed, L0_tok_b_embed, L0_tok_pos_embed, L0_attn_Wq, L0_attn_Wk,
           L0_attn_Wv, L0_attn_Wo, L0_attn_bo, L0_ffn_w_up, L0_ffn_w_down):
    import concourse.bacc as bacc
    from concourse.bass_utils import run_bass_kernel_spmd

    def contiguous(z):
        return np.ascontiguousarray(z)

    we = np.asarray(L0_tok_W_embed).reshape(6, 128, D).transpose(1, 0, 2).reshape(128, 6 * D)

    def interleaved(w):
        return w.reshape(D, 2, 8, HD).transpose(0, 1, 3, 2).reshape(D, D)

    wq, wk, wv, wo = (np.asarray(z).T for z in (L0_attn_Wq, L0_attn_Wk, L0_attn_Wv, L0_attn_Wo))
    wqkvo = np.stack([interleaved(wq), interleaved(wk), wv, wo]).reshape(4, 2, 128, D)
    wqkvo = wqkvo.transpose(2, 0, 1, 3).reshape(128, 8 * D)
    w_upT = np.asarray(L0_ffn_w_up).T.reshape(2, 128, FF).transpose(1, 0, 2).reshape(128, 2 * FF)
    w_downT = np.asarray(L0_ffn_w_down).T.reshape(NFF, 128, D).transpose(1, 0, 2).reshape(128, NFF * D)
    pos = np.asarray(L0_tok_pos_embed)[0]
    pos = np.concatenate([pos, pos[:TXT]]).reshape(2, R, D).transpose(1, 0, 2)
    arrays = {
        "x": contiguous(np.asarray(x)), "txt": contiguous(np.asarray(txt)), "w_embed": contiguous(we),
        "b_embed": contiguous(np.broadcast_to(np.asarray(L0_tok_b_embed), (R, D))),
        "pos": contiguous(pos), "wqkvo": contiguous(wqkvo),
        "bo": contiguous(np.broadcast_to(np.asarray(L0_attn_bo), (R, D))),
        "w_upT": contiguous(w_upT), "w_downT": contiguous(w_downT),
    }
    nc = bacc.Bacc("TRN2", target_bir_lowering=False, num_devices=1)
    args = [nc.dram_tensor(n, z.shape, mybir.dt.from_np(z.dtype), kind="ExternalInput").ap()
            for n, z in arrays.items()]
    out = nc.dram_tensor("out", (B, S, D), F32, kind="ExternalOutput").ap()
    build(nc, *args, out)
    r = run_bass_kernel_spmd(nc, [arrays], core_ids=[0])
    return r.results[0]["out"]
```

```python
from contextlib import ExitStack

import numpy as np
import concourse.bass as bass
from concourse import mybir

ALU = mybir.AluOpType
ACT = mybir.ActivationFunctionType
AX = mybir.AxisListType
F32 = mybir.dt.float32
F32R = mybir.dt.float32r
F16 = mybir.dt.float16
BF16 = mybir.dt.bfloat16

B, C, SIDE, PATCH = 64, 3, 224, 16
NS = SIDE // PATCH
NPATCH = NS * NS
TXT = 32
S = NPATCH + TXT
R = S // 2
RP1 = NPATCH - R
D, H, HD, FF = 256, 16, 16, 1024
NPAIR = B // 2
T2 = 2 * S
TP = 2 * NPATCH
PROWS = 2 * C * NS
PCOLS = PATCH * SIDE
NFF = FF // 128
NXG = [(0, 5), (5, 10), (10, 14)]
HS = H * S
PAD = 16
VW = 1 + 3 * HD
PARTS = [(0, 0), (0, 1), (0, 2), (1, 0), (1, 1), (2, 0)]
KS = len(PARTS) * HD
KM = KS + 3
EPS = 1e-5
RMS_EPS = 1e-8
NEG = -1e30

DENSE = ([("v", 0), ("v", 1)] + [("pix", k) for k in range(6)] + [("emb", 0), ("emb", 1), ("spare", 0)]
         + [("up", 0), ("ct", 0), ("ct", 1), ("up", 1), ("o", 0), ("o", 1), ("up", 2), ("ht", 0), ("ht", 1)]
         + [("up", m) for m in range(3, 8)] + [("xt", 0), ("xt", 1), ("qk", 0), ("ss", 0), ("dn", 0),
            ("qk", 1), ("qk", 2), ("dn", 1), ("qk", 3), ("x2t", 0), ("x2t", 1)])
PER = {"pix": 6, "emb": 2, "ct": 2, "up": 8, "o": 2, "ht": 2, "xt": 2, "qk": 4, "v": 2, "ss": 1,
       "dn": 2, "x2t": 2}
LAG = {"pix": 0, "emb": 0, "ht": 0, "xt": 0, "qk": 0, "v": 1, "ct": 2, "o": 2, "x2t": 2, "up": 3,
       "ss": 3, "dn": 3}
NDENSE = len(DENSE)
assert NDENSE % 3 == 0


def build(nc, x, txt, w_embed, b_embed, pos, wqkvo, bo, w_upT, w_downT, out):
    qk_scr = nc.dram_tensor("qk_scr", (2, 2, 2, 3, 2, 128, S), BF16, kind="Internal").ap()
    m_scr = nc.dram_tensor("m_scr", (2, 2, 48, S), BF16, kind="Internal").ap()

    with ExitStack() as ctx:
        def sb(name, shape, dt):
            return ctx.enter_context(nc.sbuf_tensor(name, shape, dt))

        def sem(name):
            return ctx.enter_context(nc.semaphore(name))

        ident = sb("ident", [128, 128], F32)
        identb = sb("identb", [128, 128], BF16)
        cmask = sb("cmask", [128, R], BF16)
        onesb = sb("onesb", [128, 2], BF16)
        posb = sb("posb", [R, 2, D], F32)
        borow = sb("borow", [R, D], F32)
        we = [sb("we_hi", [128, 6, D], F32R), sb("we_lo", [128, 6, D], F32R)]
        wa = [sb("wa_hi", [128, 4, 2, D], F32R), sb("wa_lo", [128, 4, 2, D], F32R)]
        wup = sb("wup", [128, 2, FF], BF16)
        wdn = sb("wdn", [128, NFF, D], BF16)
        tern = sb("tern", [128, 8], F32)
        pix = sb("pix", [PROWS, PCOLS], F32)
        pT = [sb("pT_hi", [128, 2, 2 * C * NPATCH], F32R), sb("pT_lo", [128, 2, 2 * C * NPATCH], F32R)]
        hT = sb("hT", [128, 2, TP], F32)
        h = sb("h", [128, 2, 4 * D], F32)
        st1 = sb("st1", [R, 4, 6], F32)
        mv1 = sb("mv1", [R, 4, 2], F32)
        rstd1 = sb("rstd1", [R, 2, 4], F32)
        exps = sb("exps", [R, 3, 4], F32)
        aT = [sb("aT_hi", [128, 2, T2], F32R), sb("aT_lo", [128, 2, T2], F32R)]
        qkp = sb("qkp", [128, 2, 3, T2], BF16)
        qkr = sb("qkr", [128, T2], F32)
        vp = sb("vp", [R, 2, 4, H, VW], BF16)
        vr = sb("vr", [R, 2 * D], F32)
        qst = [sb(f"qst{b}", [KM, HS + PAD], BF16) for b in range(2)]
        kst = [sb(f"kst{b}", [KM, HS + PAD], BF16) for b in range(2)]
        mx = sb("mx", [R, 2, 2, H], F32)
        mr = sb("mr", [R, 2, 2, H], F32)
        mp = sb("mp", [R, 2, 2, 3, H], BF16)
        mT = sb("mT", [48, 2, S], BF16)
        PW = 3 * T2 + PAD
        pr = [sb(f"pr{i}", [R, PW], F32) for i in range(2)]
        pl = [sb(f"pl{i}", [R, PW], F16) for i in range(2)]
        cu = sb("cu", [R, 2, 8, HD], F32)
        rs = sb("rs", [R, 2, 8], F32)
        cx = sb("cx", [R, 4, D], F32)
        xn = cx[:].rearrange("p j d -> p (j d)")
        h2 = sb("h2", [128, 2, 4 * D], F32)
        xn2 = sb("xn2", [R, 4 * D], F32)
        st2 = sb("st2", [R, 4, 6], F32)
        mv2 = sb("mv2", [R, 4, 2], F32)
        nb1 = sb("nb1", [R, 4], F32)
        nb2 = sb("nb2", [R, 4], F32)
        ln2 = sb("ln2", [R, 7, 4], F32)
        xT2 = [sb("xT2_hi", [128, 2, T2], F16), sb("xT2_lo", [128, 2, T2], F16)]
        g = sb("g", [128, NFF, T2], F32)
        gl = sb("gl", [128, NFF, T2], F16)
        sq = sb("sq", [128, 2, T2], F32)
        acc = sb("acc", [128, T2], F32)
        accl = sb("accl", [128, T2], F16)
        ssq = sb("ssq", [R, 4, 4], F32)
        patches = g[0:PROWS].rearrange("p a b -> p (a b)")[:, 0:PCOLS].rearrange(
            "p (h n z) -> p h n z", h=2, n=NS)
        onesf = acc[:, 0:128]
        brow = xn2[:, 0:D]

        dense = ctx.enter_context(nc.psum_tensor("dense", [128, 3, 512], F32))
        score = ctx.enter_context(nc.psum_tensor("score", [128, 3, 512], F32))
        pvps = ctx.enter_context(nc.psum_tensor("pvps", [128, 2, 512], F32))

        s_w, s_pix, s_txt = sem("s_w"), sem("s_pix"), sem("s_txt")
        s_qks = [[sem(f"s_qks{u}{i}") for i in range(2)] for u in range(2)]
        s_stack = [sem(f"s_stack{b}") for b in range(2)]
        s_ms = [sem(f"s_ms{b}") for b in range(2)]
        s_mi = [sem(f"s_mi{b}") for b in range(2)]
        s_out = sem("s_out")
        s_apart = sem("s_apart")
        pe = {n: sem("pe_" + n) for n in ["pix", "emb", "ht", "xt", "qk", "v", "s", "st", "pv", "mt",
                                          "ct", "o", "x2t", "up", "ss", "dn", "init"]}
        a = {n: sem("a_" + n) for n in ["ro", "pix", "emb", "xt", "qk0", "qk1", "v0", "v1", "exp", "mt",
                                        "ct", "x2t", "gelu", "sq", "w", "xn", "xn2"]}
        v = {n: sem("v_" + n) for n in ["pix", "h", "st1", "mv1", "nb", "xt", "qkr", "vr", "v2",
                                        "max", "m0", "mr", "m1", "m2", "pl", "cu", "ct", "h2", "st2",
                                        "mv2", "nb2", "x2t", "gl", "accl", "ss", "fin", "w"]}
        p = {n: sem("p_" + n) for n in ["mask", "pl", "gl", "qk2", "cx", "bo", "rstd1", "ln2", "acc", "ss", "w"]}

        def began(pair):
            return not isinstance(pair, int) or pair >= 0

        def count(per, pair, k):
            return (min(pair, NPAIR - 1) if isinstance(pair, int) else pair) * per + k

        def apart(eng):
            eng.sem_inc(s_apart, 1)

        released = {"pix": v["pix"], "emb": a["emb"], "ht": v["h"], "xt": v["xt"], "qk": v["qkr"],
                    "v": v["vr"], "ct": v["ct"], "o": v["h2"], "x2t": v["x2t"], "up": a["gelu"],
                    "ss": v["ss"], "dn": v["fin"]}

        def live(pair):
            return not isinstance(pair, int) or 0 <= pair < NPAIR

        def emptied(t, name, k):
            m, back = DENSE.index((name, k)) - 3, 0
            while back < 3:
                if m < 0:
                    m, back = m + NDENSE, back + 1
                other, j = DENSE[m]
                if other != "spare" and live(t - back - LAG[other]):
                    return released[other], count(PER[other], t - back - LAG[other], j + 1)
                m -= 3
            return a["w"], 1

        def stores(pair, parity, times):
            return ((min(pair, NPAIR - 1) if isinstance(pair, int) else pair) - parity) * 16 + 16 * times

        def bank_of(name, k):
            return dense[:, DENSE.index((name, k)) % 3]

        def hi_view(ap2d):
            return ap2d.bitcast(BF16)[:, 1::2]

        def col(blk, b):
            return b * S + blk * R

        def steps(body, eng):
            for t in range(4):
                body(t, t % 2)
            with eng.Fori(4, NPAIR - 2, 2) as i:
                body(i, 0)
                body(i + 1, 1)
            for t in range(NPAIR - 2, NPAIR + 3):
                body(t, t % 2)

        block = ctx.enter_context(nc.Block())

        @block.sync
        def _(sp):
            for i, (dst, src) in enumerate([
                    (g[:].rearrange("p a b -> p (a b)")[:, 0:1536], w_embed),
                    (g[:].rearrange("p a b -> p (a b)")[:, 1536:3584], wqkvo),
                    (h[:].rearrange("p a b -> p (a b)"), w_upT),
                    (h2[:].rearrange("p a b -> p (a b)"), w_downT),
                    (posb[:], pos), (brow, b_embed), (borow[:], bo)]):
                sp.dma_start(dst, src).then_inc(s_w, 16)
            xp = x.rearrange("b c (n q) w -> (b c n) (q w)", q=PATCH)

            def load_pixels(pair):
                sp.dma_start(pix[:], xp[bass.ds(pair * PROWS, PROWS), :]).then_inc(s_pix, 16)

            load_pixels(0)

            def step(t, u):
                if live(t) and (not isinstance(t, int) or t + 1 < NPAIR):
                    sp.wait_ge(a["ro"], count(2, t, 2))
                    load_pixels(t + 1)
                for b in range(2):
                    if live(t - 1):
                        if began(t - 2):
                            sp.wait_ge(pe["st"], count(24, t - 2, 12 * b + 12))
                        apart(sp)
                        for i in range(2):
                            sp.wait_ge(s_qks[1 - u][i], stores(t - 1, 1 - u, 2))
                            apart(sp)
                        for which, st in ((0, qst[b]), (1, kst[b])):
                            for j, parts in enumerate(PARTS):
                                src = qk_scr[1 - u, which, :, parts[which], b]
                                sp.dma_start(st[16 * j:16 * j + 16, 0:HS].rearrange("d (m z) -> d m z", m=2),
                                             src.rearrange("m (d e) s -> d m (e s)", d=HD)
                                             ).then_inc(s_stack[b], 16)
                if live(t):
                    if isinstance(t, int) and t < 2:
                        sp.wait_ge(v["w"], 8)
                    if began(t - 2):
                        sp.wait_ge(v["h2"], count(2, t - 2, 2))
                    apart(sp)
                    if began(t - 2):
                        sp.wait_ge(p["bo"], count(1, t - 2, 1))
                    sp.dma_start(h[RP1:R, u, 2 * D:4 * D].rearrange("p (b d) -> p b d", b=2),
                                 txt[bass.ds(t * 2, 2)].rearrange("b r d -> r b d")).then_inc(s_txt, 16)

                def maxima(b):
                    if live(t - 1):
                        sp.wait_ge(a["mt"], count(2, t - 1, b + 1))
                        sp.dma_start(m_scr[1 - u, b], mT[:, b]).then_inc(s_ms[b], 16)
                        sp.wait_ge(s_ms[b], (t - 1) * 16 + 16)
                        sp.dma_start(qst[b][KS:KM, 0:HS],
                                     m_scr[1 - u, b].rearrange("(c e) s -> c (e s)", c=3)).then_inc(s_mi[b], 16)

                def store_parts(k):
                    if live(t):
                        sp.wait_ge(p["qk2"], count(4, t, k + 1))
                        sp.dma_start(qk_scr[u, k // 2, k % 2].rearrange("c b f s -> f c b s"),
                                     qkp[:, k % 2].rearrange("p c (b s) -> p c b s", b=2)
                                     ).then_inc(s_qks[u][k % 2], 16)

                maxima(0)
                store_parts(0)
                store_parts(1)
                maxima(1)
                store_parts(2)
                store_parts(3)
                for blk in range(2):
                    if live(t - 3):
                        sp.wait_ge(v["fin"], count(2, t - 3, blk + 1))
                        sp.dma_start(out[bass.ds((t - 3) * 2, 2), blk * R:blk * R + R].rearrange("b r d -> r b d"),
                                     h2[0:R, 1 - u, 2 * D * blk:2 * D * blk + 2 * D].rearrange(
                                         "p (b d) -> p b d", b=2)).then_inc(s_out, 16)

            steps(step, sp)
            sp.wait_ge(s_out, 32 * NPAIR)

        @block.tensor
        def _(eng):
            def mm(*args, **kw):
                return nc.tensor.matmul(*args, **kw)

            def three(ps, stat, mov, start, stop):
                mm(ps, stat[0], mov[0], start=start, stop=False)
                mm(ps, stat[0], mov[1], start=False, stop=False)
                return mm(ps, stat[1], mov[0], start=False, stop=stop)

            eng.wait_ge(v["w"], 3)
            mm(dense[:, 0, 0:2], onesf, tern[:, 0:2], start=True, stop=True).then_inc(pe["init"], 1)
            eng.wait_ge(p["w"], 6)
            eng.wait_ge(v["w"], 12)

            def pixels(t, k):
                eng.wait_ge(*emptied(t, "pix", k))
                ps = bank_of("pix", k)
                ph, (n0, n1) = k // 3, NXG[k % 3]
                if k % 3 == 0:
                    eng.wait_ge(a["ro"], count(2, t, ph + 1))
                for i, n in enumerate(range(n0, n1)):
                    last = nc.tensor.transpose(ps[:, i * PROWS:(i + 1) * PROWS],
                                               patches[:, ph, n], ident[0:PROWS, 0:PROWS])
                last.then_inc(pe["pix"], 1)

            def embed(t, m, ph):
                if ph == 0:
                    eng.wait_ge(*emptied(t, "emb", m))
                eng.wait_ge(v["pix"], count(6, t, 3 * ph + 3))
                o = bank_of("emb", m)[:, 0:TP].rearrange("p (b n) -> p b n", b=2)
                for c in range(C):
                    mov = [q[:, ph].rearrange("p (b c n) -> p b c n", b=2, c=C)[:, :, c] for q in pT]
                    stat = [w[:, 2 * c + ph, m * 128:m * 128 + 128] for w in we]
                    last = three(o, stat, mov, ph == 0 and c == 0, ph == 1 and c == 2)
                if ph == 1:
                    last.then_inc(pe["emb"], 1)

            def hidden_rows(t, blk):
                eng.wait_ge(*emptied(t, "ht", blk))
                ps = bank_of("ht", blk)
                if blk == 0:
                    eng.wait_ge(a["emb"], count(2, t, 2))
                w = R if blk == 0 else RP1
                for b in range(2):
                    for m in range(2):
                        c0 = b * NPATCH + blk * R
                        last = nc.tensor.transpose(ps[0:w, b * D + m * 128:b * D + m * 128 + 128],
                                                   hT[:, m, c0:c0 + w], ident[:])
                last.then_inc(pe["ht"], 1)

            def to_columns(t, name, m, src):
                eng.wait_ge(*emptied(t, name, m))
                ps = bank_of(name, m)
                for blk in range(2):
                    for b in range(2):
                        c0 = (2 * blk + b) * D + m * 128
                        last = nc.tensor.transpose(ps[:, col(blk, b):col(blk, b) + R], src[:, c0:c0 + 128],
                                                   ident[0:R, 0:R])
                last.then_inc(pe[name], 1)

            def queries_keys(t, k):
                eng.wait_ge(*emptied(t, "qk", k))
                ps = bank_of("qk", k)
                if k == 0:
                    eng.wait_ge(v["xt"], count(2, t, 2))
                for c in range(2):
                    last = three(ps[:, 0:T2], [w[:, k // 2, c, (k % 2) * 128:(k % 2) * 128 + 128] for w in wa],
                                 [q[:, c] for q in aT], c == 0, c == 1)
                last.then_inc(pe["qk"], 1)

            def token_product(t, name, blk, wi):
                eng.wait_ge(*emptied(t, name, blk))
                ps = bank_of(name, blk)
                for b in range(2):
                    for c in range(2):
                        last = three(ps[0:R, b * D:b * D + D],
                                     [q[:, c, col(blk, b):col(blk, b) + R] for q in aT],
                                     [w[:, wi, c] for w in wa], c == 0, c == 1)
                last.then_inc(pe[name], 1)

            def up(t, m):
                eng.wait_ge(*emptied(t, "up", m))
                ps = bank_of("up", m)
                if m == 0:
                    eng.wait_ge(v["x2t"], count(2, t - 3, 2))
                for c in range(2):
                    for i in range(2):
                        last = mm(ps[:, 0:T2], wup[:, c, m * 128:m * 128 + 128], xT2[i][:, c],
                                  start=(c == 0 and i == 0), stop=(c == 1 and i == 1))
                last.then_inc(pe["up"], 1)

            def sum_squares(t):
                eng.wait_ge(*emptied(t, "ss", 0))
                ps = bank_of("ss", 0)
                eng.wait_ge(v["accl"], count(1, t - 3, 1))
                for j in range(4):
                    c0 = col(j // 2, j % 2)
                    mm(ps[0:R, j:j + 1], hi_view(acc[:, c0:c0 + R]), onesb[:, 0:1], start=True, stop=False)
                    last = mm(ps[0:R, j:j + 1], accl[:, c0:c0 + R], onesb[:, 0:1], start=False, stop=True)
                last.then_inc(pe["ss"], 1)

            def down(t, blk, part):
                if part == 0:
                    eng.wait_ge(*emptied(t, "dn", blk))
                    if blk == 0:
                        eng.wait_ge(v["gl"], count(5, t - 3, 5))
                        eng.wait_ge(p["gl"], count(3, t - 3, 3))
                b = part // 2
                c0 = col(blk, b)
                ps = bank_of("dn", blk)[0:R, b * D:b * D + D]
                for m in range(4 * (part % 2), 4 * (part % 2) + 4):
                    mm(ps, hi_view(g[:, m, c0:c0 + R]), wdn[:, m], start=(m == 0), stop=False)
                    last = mm(ps, gl[:, m, c0:c0 + R], wdn[:, m], start=False, stop=(m == NFF - 1))
                if part == 3:
                    last.then_inc(pe["dn"], 1)

            def heads_of(n):
                g4, k = divmod(n, 3)
                return (range(4 * g4, 4 * g4 + 4), False) if k == 2 else (range(4 * g4 + 2 * k, 4 * g4 + 2 * k + 2), True)

            def scores_columns(t, n):
                b, k = divmod(n, 12)
                if k == 0:
                    eng.wait_ge(s_mi[b], count(16, t - 2, 16))
                if n >= 3:
                    eng.wait_ge(a["exp"], count(24, t - 2, n - 2))
                elif live(t - 2) and not (isinstance(t, int) and t < 2):
                    eng.wait_ge(v["max"], count(24, t - 2, 24 - 2 + n))
                heads, both = heads_of(k)
                for i, hd in enumerate(heads):
                    c0 = hd * S + (0 if both else R)
                    w = S if both else R
                    last = mm(score[:, n % 3, i * w:i * w + w], kst[b][0:KM, c0:c0 + 128],
                              qst[b][0:KM, c0:c0 + w], start=True, stop=True)
                last.then_inc(pe["st"], 1)

            def scores_rows(t, n):
                b, k = divmod(n, 12)
                if k == 0:
                    eng.wait_ge(s_stack[b], count(192, t - 1, 192))
                if n >= 3:
                    eng.wait_ge(v["max"], count(24, t - 1, n - 2))
                elif live(t - 2):
                    if began(t - 2):
                        eng.wait_ge(a["exp"], count(24, t - 2, 24 - 2 + n))
                heads, both = heads_of(k)
                w = S if both else R
                for i, hd in enumerate(heads):
                    c0 = hd * S + (R if both else 0)
                    mm(score[:, n % 3, i * w:i * w + w], qst[b][0:KS, c0:c0 + 128],
                       kst[b][0:KS, hd * S:hd * S + w], start=(i == 0), stop=False, skip_group_check=True)
                nh = len(heads)
                o = score[:, n % 3, 0:T2].rearrange("p (i w) -> p i w", i=nh)[:, :, w - R:w]
                last = mm(o, identb[0:R, :], cmask[0:R].rearrange("p (o w) -> p o w", o=1).broadcast_to([R, nh, R]),
                          start=False, stop=True, skip_group_check=True)
                last.then_inc(pe["s"], 1)

            def weighted_values(t, u, gi):
                b, g4 = divmod(gi, 4)
                eng.wait_ge(v["pl"], count(8, t - 2, gi + 1))
                eng.wait_ge(p["pl"], count(8, t - 2, gi + 1))
                if gi == 0:
                    eng.wait_ge(v["v2"], count(2, t - 2, 2))
                if gi >= 2:
                    eng.wait_ge(v["cu"], count(8, t - 2, gi - 1))
                else:
                    eng.wait_ge(a["mt"], count(2, t - 2, gi + 1))
                P_, L_ = pr[gi % 2], pl[gi % 2]
                for qb in range(2):
                    for i in range(4):
                        hd = 4 * g4 + i
                        o = pvps[:, gi % 2, (4 * qb + i) * VW:(4 * qb + i) * VW + VW]
                        for kb in range(qb + 1):
                            c0 = i * S + qb * R if kb == 0 else 2 * T2 + i * R
                            val = vp[:, u, 2 * kb + b, hd]
                            mm(o, hi_view(P_[:, c0:c0 + 128]), val, start=(kb == 0), stop=False)
                            last = mm(o[:, 0:1 + 2 * HD], L_[:, c0:c0 + 128], val[:, 0:1 + 2 * HD],
                                      start=False, stop=(kb == qb))
                last.then_inc(pe["pv"], 1)

            def maxima_rows(t, b):
                eng.wait_ge(v["m2"], count(2, t - 1, b + 1))
                if live(t - 2):
                    if began(t - 2):
                        eng.wait_ge(v["cu"], count(8, t - 2, 7 + b))
                apart(eng)
                for qb in range(2):
                    last = nc.tensor.transpose(pvps[0:48, b, 0:256].bitcast(BF16)[:, qb * R:qb * R + R],
                                               mp[:, b, qb].rearrange("p c e -> p (c e)"), identb[0:R, 0:R])
                last.then_inc(pe["mt"], 1)

            def step(t, u):
                A, Bm, Cc, Dd = live(t), live(t - 1), live(t - 2), live(t - 3)
                for gi in range(9):
                    if Cc and gi < 8:
                        for n in range(3):
                            scores_columns(t, 3 * gi + n)
                    if Bm and gi < 2:
                        token_product(t, "v", gi, 2)
                    if A and 2 <= gi < 5:
                        pixels(t, 2 * gi - 4)
                        pixels(t, 2 * gi - 3)
                    if A and gi >= 5:
                        embed(t, (gi - 5) // 2, (gi - 5) % 2)
                    if Cc and gi >= 1:
                        weighted_values(t, u, gi - 1)
                for n in range(24):
                    if Bm:
                        scores_rows(t, n)
                    if Bm and n == 14:
                        maxima_rows(t, 0)
                    if Dd and n in (0, 2, 5, 7, 8, 9, 10, 11):
                        up(t, (0, 2, 5, 7, 8, 9, 10, 11).index(n))
                    if Cc and n == 1:
                        eng.wait_ge(p["cx"], count(8, t - 2, 8))
                        to_columns(t, "ct", 0, xn)
                        to_columns(t, "ct", 1, xn)
                    if Cc and n == 3:
                        eng.wait_ge(v["ct"], count(2, t - 2, 2))
                    if Cc and n in (3, 4):
                        token_product(t, "o", n - 3, 3)
                    if A and n == 6:
                        hidden_rows(t, 0)
                        hidden_rows(t, 1)
                    if A and n == 13:
                        eng.wait_ge(a["xn"], count(4, t, 4))
                        to_columns(t, "xt", 0, xn)
                        to_columns(t, "xt", 1, xn)
                    if A and n in (14, 17, 20, 23):
                        queries_keys(t, (n - 14) // 3)
                    if Dd and n == 15:
                        sum_squares(t)
                    if Dd and n in (15, 16, 18, 19):
                        down(t, 0, (15, 16, 18, 19).index(n))
                    if Dd and n in (21, 22):
                        down(t, 1, n - 21)
                if Dd:
                    down(t, 1, 2)
                    down(t, 1, 3)
                if Bm:
                    maxima_rows(t, 1)
                if Cc:
                    eng.wait_ge(a["xn2"], count(4, t - 2, 4))
                    to_columns(t, "x2t", 0, xn2[:])
                    to_columns(t, "x2t", 1, xn2[:])

            steps(step, eng)

        @block.scalar
        def _(eng):
            act = nc.scalar.activation
            gf = g[:].rearrange("p a b -> p (a b)")
            eng.wait_ge(s_w, 16 * 7)
            act(we[0][:].rearrange("p a b -> p (a b)"), gf[:, 0:1536], ACT.Copy).then_inc(a["w"], 1)
            act(wa[0][:].rearrange("p a b c -> p (a b c)"), gf[:, 1536:3584], ACT.Copy).then_inc(a["w"], 1)

            def reorder(t, ph):
                if ph == 0:
                    eng.wait_ge(s_pix, count(16, t, 16))
                    if began(t - 4):
                        eng.wait_ge(pe["dn"], count(2, t - 4, 2))
                    if isinstance(t, int) and t == 0:
                        eng.wait_ge(v["w"], 11)
                half = PCOLS // 2
                act(patches[:, ph].rearrange("p n (q w) -> p q n w", q=8),
                    pix[:, ph * half:ph * half + half].rearrange("p (q n w) -> p q n w", q=8, n=NS),
                    ACT.Copy).then_inc(a["ro"], 1)

            def pixels_hi(t, k):
                n0, n1 = NXG[k % 3]
                eng.wait_ge(pe["pix"], count(6, t, k + 1))
                if k == 0:
                    if began(t - 1):
                        eng.wait_ge(pe["emb"], count(2, t - 1, 2))
                src = bank_of("pix", k)[:, 0:(n1 - n0) * PROWS].rearrange("p (n r) -> p r n", r=PROWS)
                dst = pT[0][:, k // 3].rearrange("p (r n) -> p r n", n=NS)[:, :, n0:n1]
                act(dst, src, ACT.Copy).then_inc(a["pix"], 1)

            def hi_part(t, name, m, dst, pair):
                eng.wait_ge(pe[name], count(2, pair, m + 1))
                act(dst[:, m], bank_of(name, m)[:, 0:T2], ACT.Copy).then_inc(a[name], 1)

            def exponentials(t, gi):
                Pb = pr[gi % 2]
                if gi >= 2:
                    eng.wait_ge(pe["pv"], count(8, t - 2, gi - 1))
                else:
                    if began(t - 3):
                        eng.wait_ge(pe["pv"], count(8, t - 3, 7 + gi))
                for k in range(3):
                    n = 3 * gi + k
                    eng.wait_ge(pe["st"], count(24, t - 2, n + 1))
                    act(Pb[:, k * T2:k * T2 + T2], score[0:R, n % 3, 0:T2], ACT.Exp,
                        scale=float(HD) ** -0.5).then_inc(a["exp"], 1)

            def gelu(t, m):
                eng.wait_ge(pe["up"], count(8, t - 3, m + 1))
                if m == 0:
                    if began(t - 4):
                        eng.wait_ge(pe["dn"], count(2, t - 4, 2))
                    eng.wait_ge(pe["pix"], count(6, t, 6))
                act(g[:, m], bank_of("up", m)[:, 0:T2], ACT.Gelu).then_inc(a["gelu"], 1)
                eng.wait_ge(a["gelu"], count(8, t - 3, m + 1))
                if m >= 2:
                    eng.wait_ge(p["acc"], count(7, t - 3, max(1, m - 2)))
                else:
                    if began(t - 4):
                        eng.wait_ge(p["acc"], count(7, t - 4, 7))
                act(sq[:, m % 2], g[:, m], ACT.Square).then_inc(a["sq"], 1)

            def part_qk(t, u, k):
                eng.wait_ge(pe["qk"], count(4, t, k + 1))
                if k >= 2:
                    eng.wait_ge(s_qks[u][k % 2], stores(t, u, 1))
                else:
                    if began(t - 1):
                        eng.wait_ge(s_qks[1 - u][k % 2], stores(t - 1, 1 - u, 2))
                act(qkp[:, k % 2, 0], bank_of("qk", k)[:, 0:T2], ACT.Copy).then_inc(a["qk0"], 1)
                eng.wait_ge(v["qkr"], count(4, t, k + 1))
                act(qkp[:, k % 2, 1], qkr[:], ACT.Copy).then_inc(a["qk1"], 1)

            def value_part(t, u, blk, i):
                dst = vp[:, 1 - u, 2 * blk:2 * blk + 2].rearrange("p b e c -> p (b e) c")[:, :, 1 + HD * i:1 + HD * i + HD]
                if i == 0:
                    eng.wait_ge(pe["v"], count(2, t - 1, blk + 1))
                    if blk == 0:
                        if began(t - 3):
                            eng.wait_ge(pe["pv"], count(8, t - 3, 8))
                    act(dst, bank_of("v", blk)[0:R, 0:2 * D].rearrange("p (e c) -> p e c", c=HD),
                        ACT.Copy).then_inc(a["v0"], 1)
                else:
                    eng.wait_ge(v["vr"], count(2, t - 1, blk + 1))
                    act(dst, vr[:].rearrange("p (e c) -> p e c", c=HD), ACT.Copy).then_inc(a["v1"], 1)

            def normalized(t, src, dst, scale, bias, s_out_, s_bias, pair):
                eng.wait_ge(s_bias, count(1, pair, 1))
                for j in range(4):
                    act(dst[:, j * D:j * D + D], src[:, j * D:j * D + D], ACT.Identity,
                        bias=bias[:, j:j + 1], scale=scale[:, j:j + 1]).then_inc(s_out_, 1)

            def maxima(t, b):
                eng.wait_ge(pe["mt"], count(2, t - 1, b + 1))
                if began(t - 2):
                    eng.wait_ge(s_ms[b], count(16, t - 2, 16))
                act(mT[:, b], pvps[0:48, b, 0:256].bitcast(BF16)[:, 0:S], ACT.Copy).then_inc(a["mt"], 1)

            def step(t, u):
                A, Bm, Cc, Dd = live(t), live(t - 1), live(t - 2), live(t - 3)
                for gi in range(10):
                    if Cc and gi < 8:
                        exponentials(t, gi)
                    if Bm and 1 <= gi < 3:
                        value_part(t, u, gi - 1, 1)
                    if Bm and gi < 2:
                        value_part(t, u, gi, 0)
                    if A and gi < 2:
                        reorder(t, gi)
                    if A and 2 <= gi < 5:
                        pixels_hi(t, 2 * gi - 4)
                        pixels_hi(t, 2 * gi - 3)
                    if A and gi in (7, 9):
                        m = (gi - 7) // 2
                        eng.wait_ge(pe["emb"], count(2, t, m + 1))
                        if m == 0:
                            if began(t - 1):
                                eng.wait_ge(pe["ht"], count(2, t - 1, 2))
                        act(hT[:, m], bank_of("emb", m)[:, 0:TP], ACT.Copy).then_inc(a["emb"], 1)
                for n in range(24):
                    if Dd and n in (0, 2, 5, 7, 8, 9, 10, 11):
                        gelu(t, (0, 2, 5, 7, 8, 9, 10, 11).index(n))
                    if Cc and n == 1:
                        if began(t - 1):
                            eng.wait_ge(pe["v"], count(2, t - 1, 2))
                        hi_part(t, "ct", 0, aT[0], t - 2)
                        hi_part(t, "ct", 1, aT[0], t - 2)
                    if A and n == 11:
                        if began(t - 1):
                            eng.wait_ge(pe["xt"], count(2, t - 1, 2))
                        if began(t - 2):
                            eng.wait_ge(pe["ct"], count(2, t - 2, 2))
                        normalized(t, h[0:R, u], xn, rstd1[:, 1], nb1, a["xn"], v["nb"], t)
                    if A and n == 13:
                        if began(t - 2):
                            eng.wait_ge(pe["o"], count(2, t - 2, 2))
                        hi_part(t, "xt", 0, aT[0], t)
                        hi_part(t, "xt", 1, aT[0], t)
                    if Cc and n == 13:
                        if began(t - 3):
                            eng.wait_ge(pe["x2t"], count(2, t - 3, 2))
                        normalized(t, h2[0:R, u], xn2, ln2[:, 4], nb2, a["xn2"], v["nb2"], t - 2)
                    if A and n in (14, 17, 20, 23):
                        part_qk(t, u, (n - 14) // 3)
                    if Bm and n == 14:
                        maxima(t, 0)
                if Bm:
                    maxima(t, 1)
                if Cc:
                    if began(t - 3):
                        eng.wait_ge(pe["up"], count(8, t - 3, 8))
                    hi_part(t, "x2t", 0, xT2[0], t - 2)
                    hi_part(t, "x2t", 1, xT2[0], t - 2)

            steps(step, eng)

        @block.vector
        def _(eng):
            tt, ts = nc.vector.tensor_tensor, nc.vector.tensor_scalar
            gf = g[:].rearrange("p a b -> p (a b)")
            hf, h2f = h[:].rearrange("p a b -> p (a b)"), h2[:].rearrange("p a b -> p (a b)")
            eng.memset(onesb[:], 1.0)
            for i, e in enumerate((-0.5, 0.5, -1.0)):
                eng.memset(exps[:, i], e)
            for b in range(2):
                eng.memset(qst[b][:, HS:], 0.0)
                eng.memset(kst[b][:, HS:], 0.0)
                eng.memset(kst[b][KS:KM, 0:HS], 1.0)
                eng.memset(pr[b][:, 3 * T2:], 0.0)
                eng.memset(pl[b][:, 3 * T2:], 0.0)
            eng.memset(vp[:, :, :, :, 0:1].rearrange("p u j e c -> p (u j e) c"), 1.0)
            eng.memset(onesf, 1.0).then_inc(v["w"], 1)
            eng.wait_ge(s_w, 16 * 7)
            nc.vector.tensor_reduce(tern[:, 0:1], hf, AX.X, ALU.add, apply_absolute_value=True).then_inc(v["w"], 1)
            nc.vector.tensor_reduce(tern[:, 1:2], h2f, AX.X, ALU.add, apply_absolute_value=True).then_inc(v["w"], 1)
            eng.wait_ge(pe["init"], 1)
            ts(tern[:, 2:4], dense[:, 0, 0:2], 0.5 / (D * FF), None, ALU.mult).then_inc(v["w"], 1)
            ts(tern[:, 4:6], dense[:, 0, 0:2], -0.5 / (D * FF), None, ALU.mult).then_inc(v["w"], 1)
            eng.wait_ge(v["w"], 5)
            for i, (src, dst) in enumerate(((hf, wup[:].rearrange("p a b -> p (a b)")),
                                            (h2f, wdn[:].rearrange("p a b -> p (a b)")))):
                below = pT[0][:].bitcast(F32).rearrange("p a b -> p (a b)")[:, 0:2048] if False else gf[:, 0:2048]
                if i == 0:
                    eng.wait_ge(a["w"], 2)
                    tt(we[1][:].rearrange("p a b -> p (a b)"), gf[:, 0:1536],
                       we[0][:].bitcast(F32).rearrange("p a b -> p (a b)"), ALU.subtract).then_inc(v["w"], 1)
                    tt(wa[1][:].rearrange("p a b c -> p (a b c)"), gf[:, 1536:3584],
                       wa[0][:].bitcast(F32).rearrange("p a b c -> p (a b c)"), ALU.subtract).then_inc(v["w"], 1)
                    eng.wait_ge(v["w"], 7)
                else:
                    eng.wait_ge(v["w"], 9)
                ts(below, src, tern[:, 4 + i:5 + i], None, ALU.is_lt).then_inc(v["w"], 1)
                if i == 0:
                    eng.wait_ge(v["w"], 8)
                else:
                    eng.wait_ge(v["w"], 10)
                nc.vector.scalar_tensor_tensor(out=dst, in0=src, scalar=tern[:, 2 + i:3 + i], in1=below,
                                               op0=ALU.is_gt, op1=ALU.subtract).then_inc(v["w"], 1)
            tt(posb[:], posb[:], brow.rearrange("p (o d) -> p o d", o=1).broadcast_to([R, 2, D]),
               ALU.add).then_inc(v["w"], 1)
            eng.wait_ge(v["w"], 12)

            def pixels_lo(t, k):
                n0, n1 = NXG[k % 3]
                eng.wait_ge(a["pix"], count(6, t, k + 1))
                src = bank_of("pix", k)[:, 0:(n1 - n0) * PROWS].rearrange("p (n r) -> p r n", r=PROWS)
                hi, lo = [q[:, k // 3].rearrange("p (r n) -> p r n", n=NS)[:, :, n0:n1] for q in
                          (pT[0][:].bitcast(F32), pT[1])]
                tt(lo, src, hi, ALU.subtract).then_inc(v["pix"], 1)

            def lo_part(name, m, hi, lo, pair):
                eng.wait_ge(a[name], count(2, pair, m + 1))
                tt(lo[:, m], bank_of(name, m)[:, 0:T2], hi[:, m], ALU.subtract).then_inc(v[name], 1)

            def remainders(t, gi):
                eng.wait_ge(p["mask"], count(16, t - 2, 2 * gi + 1))
                if gi >= 2:
                    eng.wait_ge(pe["pv"], count(8, t - 2, gi - 1))
                else:
                    if began(t - 3):
                        eng.wait_ge(pe["pv"], count(8, t - 3, 7 + gi))
                Pb = pr[gi % 2][:, 0:2 * T2]
                tt(pl[gi % 2][:, 0:2 * T2], Pb, hi_view(Pb), ALU.subtract).then_inc(v["pl"], 1)

            def collect(t, gi):
                eng.wait_ge(pe["pv"], count(8, t - 2, gi + 1))
                if gi >= 2:
                    eng.wait_ge(p["cx"], count(8, t - 2, gi - 1))
                else:
                    if began(t - 3):
                        eng.wait_ge(p["cx"], count(8, t - 3, 7 + gi))
                bank = pvps[0:R, gi % 2, 0:8 * VW].rearrange("p (e c) -> p e c", c=VW)
                nc.vector.reciprocal(rs[:, gi % 2], bank[:, :, 0:1].rearrange("p e c -> p (e c)"))
                nc.vector.tensor_reduce(cu[:, gi % 2], bank[:, :, 1:VW].rearrange("p e (k d) -> p e d k", k=3),
                                        AX.X, ALU.add).then_inc(v["cu"], 1)

            def gelu_lo(t, m):
                eng.wait_ge(a["gelu"], count(8, t - 3, m + 1))
                if m == 1:
                    if began(t - 4):
                        eng.wait_ge(pe["dn"], count(2, t - 4, 2))
                tt(gl[:, m], g[:, m], hi_view(g[:, m]), ALU.subtract).then_inc(v["gl"], 1)

            def residual(t, u, blk):
                eng.wait_ge(pe["o"], count(2, t - 2, blk + 1))
                if blk == 0:
                    if began(t - 4):
                        eng.wait_ge(s_out, count(32, t - 4, 32))
                    eng.wait_ge(p["bo"], count(1, t - 2, 1))
                w = slice(2 * D * blk, 2 * D * blk + 2 * D)
                tt(h2[0:R, u, w], bank_of("o", blk)[0:R, 0:2 * D], h[0:R, u, w], ALU.add).then_inc(v["h2"], 1)

            def moments(src, st, mv, s_st, s_mv, pair):
                for j in range(4):
                    eng.bn_stats(st[:, j], src[:, j * D:j * D + D]).then_inc(s_st, 1)
                eng.wait_ge(s_st, count(4, pair, 4))
                apart(eng)
                for j in range(4):
                    eng.bn_aggr(mv[:, j], st[:, j]).then_inc(s_mv, 1)

            def maxima_unit(t, n):
                b, k = divmod(n, 12)
                g4, j = divmod(k, 3)
                eng.wait_ge(pe["s"], count(24, t - 1, n + 1))
                qb, h0, nh = (0, 4 * g4, 4) if j == 2 else (1, 4 * g4 + 2 * j, 2)
                if n == 0:
                    if began(t - 2):
                        eng.wait_ge(v["m2"], count(2, t - 2, 2))
                nc.vector.tensor_reduce(mx[:, b, qb, h0:h0 + nh],
                                        score[0:R, n % 3, 0:T2].rearrange("p (i w) -> p i w", i=nh),
                                        AX.X, ALU.max).then_inc(v["max"], 1)

            def maxima_parts(t, b):
                eng.wait_ge(v["max"], count(24, t - 1, 12 * b + 12))
                if began(t - 2):
                    eng.wait_ge(pe["mt"], count(2, t - 2, b + 1))
                part = [mp[:, b, :, i] for i in range(3)]
                ts(part[0], mx[:, b], -1.0, None, ALU.mult).then_inc(v["m0"], 1)
                eng.wait_ge(v["m0"], count(2, t - 1, b + 1))
                nc.vector.scalar_tensor_tensor(out=mr[:, b], in0=mx[:, b], scalar=-1.0, in1=part[0],
                                               op0=ALU.mult, op1=ALU.subtract).then_inc(v["mr"], 1)
                eng.wait_ge(v["mr"], count(2, t - 1, b + 1))
                nc.vector.tensor_copy(part[1], mr[:, b]).then_inc(v["m1"], 1)
                eng.wait_ge(v["m1"], count(2, t - 1, b + 1))
                tt(part[2], mr[:, b], part[1], ALU.subtract).then_inc(v["m2"], 1)

            def hidden(t, u, blk):
                eng.wait_ge(pe["ht"], count(2, t, blk + 1))
                if blk == 0:
                    if began(t - 2):
                        eng.wait_ge(v["h2"], count(2, t - 2, 2))
                w = R if blk == 0 else RP1
                tt(h[0:w, u, 2 * D * blk:2 * D * blk + 2 * D].rearrange("p (b d) -> p b d", b=2),
                   bank_of("ht", blk)[0:w].rearrange("p (b d) -> p b d", b=2),
                   posb[0:w, blk].rearrange("p (o d) -> p o d", o=1).broadcast_to([w, 2, D]),
                   ALU.add).then_inc(v["h"], 1)

            def qk_rest(t, k):
                eng.wait_ge(a["qk0"], count(4, t, k + 1))
                if k or began(t - 1):
                    eng.wait_ge(p["qk2"], count(4, t, k))
                tt(qkr[:], bank_of("qk", k)[:, 0:T2], qkp[:, k % 2, 0], ALU.subtract).then_inc(v["qkr"], 1)

            def value_rest(t, u, blk, i):
                dst = [vp[:, 1 - u, 2 * blk:2 * blk + 2].rearrange("p b e c -> p (b e) c")[:, :, 1 + HD * k:1 + HD * k + HD]
                       for k in range(3)]
                r3 = vr[:].rearrange("p (e c) -> p e c", c=HD)
                if i == 0:
                    eng.wait_ge(a["v0"], count(2, t - 1, blk + 1))
                    if blk or began(t - 2):
                        eng.wait_ge(v["v2"], count(2, t - 1, blk))
                    tt(r3, bank_of("v", blk)[0:R, 0:2 * D].rearrange("p (e c) -> p e c", c=HD), dst[0],
                       ALU.subtract).then_inc(v["vr"], 1)
                else:
                    eng.wait_ge(a["v1"], count(2, t - 1, blk + 1))
                    tt(dst[2], r3, dst[1], ALU.subtract).then_inc(v["v2"], 1)

            def bias_of(mv, rstd, nb, s_rstd, per, s_nb, pair):
                eng.wait_ge(s_rstd, count(per, pair, per))
                nc.vector.scalar_tensor_tensor(out=nb[:], in0=mv[:, :, 0:1].rearrange("p j o -> p (j o)"),
                                               scalar=-1.0, in1=rstd, op0=ALU.mult,
                                               op1=ALU.mult).then_inc(s_nb, 1)

            def final(t, blk, u):
                eng.wait_ge(pe["dn"], count(2, t - 3, blk + 1))
                if blk == 0:
                    eng.wait_ge(p["ss"], count(3, t - 3, 3))
                for b in range(2):
                    w = slice((2 * blk + b) * D, (2 * blk + b + 1) * D)
                    last = nc.vector.scalar_tensor_tensor(
                        out=h2[0:R, 1 - u, w], in0=bank_of("dn", blk)[0:R, b * D:b * D + D],
                        scalar=ssq[:, 2, 2 * blk + b:2 * blk + b + 1], in1=h2[0:R, 1 - u, w],
                        op0=ALU.mult, op1=ALU.add)
                last.then_inc(v["fin"], 1)

            def step(t, u):
                A, Bm, Cc, Dd = live(t), live(t - 1), live(t - 2), live(t - 3)
                for gi in range(9):
                    if Bm and 1 <= gi < 3:
                        value_rest(t, u, gi - 1, 1)
                    if Bm and gi < 2:
                        value_rest(t, u, gi, 0)
                    if A and 2 <= gi < 5:
                        pixels_lo(t, 2 * gi - 4)
                        pixels_lo(t, 2 * gi - 3)
                    if Cc and gi >= 1:
                        collect(t, gi - 1)
                    if Cc and gi < 8:
                        remainders(t, gi)
                for n in range(24):
                    if Bm:
                        maxima_unit(t, n)
                    if Bm and n == 12:
                        maxima_parts(t, 0)
                    if Dd and n in (2, 7, 9, 10, 11):
                        gelu_lo(t, (0, 2, 5, 7, 8, 9, 10, 11).index(n))
                    if Cc and n == 1:
                        lo_part("ct", 0, aT[0][:].bitcast(F32), aT[1], t - 2)
                        lo_part("ct", 1, aT[0][:].bitcast(F32), aT[1], t - 2)
                    if Cc and n in (3, 4):
                        residual(t, u, n - 3)
                    if Cc and n == 5:
                        eng.wait_ge(v["h2"], count(2, t - 2, 2))
                        if began(t - 3):
                            eng.wait_ge(v["nb2"], count(1, t - 3, 1))
                        if began(t - 3):
                            eng.wait_ge(p["ln2"], count(7, t - 3, 7))
                        moments(h2[0:R, u], st2, mv2, v["st2"], v["mv2"], t - 2)
                    if A and n == 6:
                        hidden(t, u, 0)
                        hidden(t, u, 1)
                        eng.wait_ge(v["h"], count(2, t, 2))
                        eng.wait_ge(s_txt, count(16, t, 16))
                        if began(t - 1):
                            eng.wait_ge(v["nb"], count(1, t - 1, 1))
                        if began(t - 1):
                            eng.wait_ge(p["rstd1"], count(2, t - 1, 2))
                        moments(h[0:R, u], st1, mv1, v["st1"], v["mv1"], t)
                    if A and n == 9:
                        if began(t - 1):
                            eng.wait_ge(a["xn"], count(4, t - 1, 4))
                        bias_of(mv1, rstd1[:, 1], nb1, p["rstd1"], 2, v["nb"], t)
                    if Cc and n == 12:
                        if began(t - 3):
                            eng.wait_ge(a["xn2"], count(4, t - 3, 4))
                        bias_of(mv2, ln2[:, 4], nb2, p["ln2"], 7, v["nb2"], t - 2)
                    if A and n == 13:
                        lo_part("xt", 0, aT[0][:].bitcast(F32), aT[1], t)
                        lo_part("xt", 1, aT[0][:].bitcast(F32), aT[1], t)
                    if A and n in (14, 17, 20, 23):
                        qk_rest(t, (n - 14) // 3)
                    if Dd and n == 14:
                        eng.wait_ge(p["acc"], count(7, t - 3, 7))
                        if began(t - 4):
                            eng.wait_ge(pe["ss"], count(1, t - 4, 1))
                        tt(accl[:], acc[:], hi_view(acc[:]), ALU.subtract).then_inc(v["accl"], 1)
                    if Dd and n == 16:
                        eng.wait_ge(pe["ss"], count(1, t - 3, 1))
                        if began(t - 4):
                            eng.wait_ge(p["ss"], count(3, t - 4, 3))
                        ts(ssq[:, 0], bank_of("ss", 0)[0:R, 0:4], 1.0 / FF, None, ALU.mult).then_inc(v["ss"], 1)
                    if Dd and n == 20:
                        final(t, 0, u)
                if Bm:
                    maxima_parts(t, 1)
                if Dd:
                    final(t, 1, u)
                if Cc:
                    lo_part("x2t", 0, xT2[0], xT2[1], t - 2)
                    lo_part("x2t", 1, xT2[0], xT2[1], t - 2)

            steps(step, eng)

        @block.gpsimd
        def _(eng):
            tt, ts = nc.gpsimd.tensor_tensor, nc.gpsimd.tensor_scalar
            for idn in (ident, identb):
                eng.memset(idn[:], 0.0).then_inc(p["w"], 1)
            eng.memset(cmask[:], 0.0).then_inc(p["w"], 1)
            eng.wait_ge(p["w"], 3)
            for idn in (ident, identb):
                nc.gpsimd.affine_select(out=idn[:], in_=idn[:], compare_op=ALU.not_equal, fill=1.0, base=0,
                                        pattern=[[-1, 128]], channel_multiplier=1).then_inc(p["w"], 1)
            nc.gpsimd.affine_select(out=cmask[:], in_=cmask[:], compare_op=ALU.is_ge, fill=NEG, base=0,
                                    pattern=[[-1, R]], channel_multiplier=1).then_inc(p["w"], 1)
            eng.wait_ge(v["w"], 1)

            def causal(t, gi):
                Pb = pr[gi % 2]
                both = Pb[:, 0:2 * T2].rearrange("p (e w) -> p e w", e=4)[:, :, 0:R]
                one = Pb[:, 2 * T2:3 * T2].rearrange("p (e w) -> p e w", e=4)
                for k, blocks in enumerate((both, one)):
                    eng.wait_ge(a["exp"], count(24, t - 2, 3 * gi + 2 + k))
                    apart(eng)
                    nc.gpsimd.affine_select(out=blocks, in_=blocks, compare_op=ALU.is_ge, fill=0.0, base=0,
                                            pattern=[[0, 4], [1, R]], channel_multiplier=-1).then_inc(p["mask"], 1)
                eng.wait_ge(p["mask"], count(16, t - 2, 2 * gi + 2))
                if gi >= 2:
                    eng.wait_ge(pe["pv"], count(8, t - 2, gi - 1))
                else:
                    if began(t - 3):
                        eng.wait_ge(pe["pv"], count(8, t - 3, 7 + gi))
                w = slice(2 * T2, 3 * T2)
                tt(pl[gi % 2][:, w], Pb[:, w], hi_view(Pb[:, w]), ALU.subtract).then_inc(p["pl"], 1)

            def gelu_lo(t, m):
                eng.wait_ge(a["gelu"], count(8, t - 3, m + 1))
                if m == 0:
                    if began(t - 4):
                        eng.wait_ge(pe["dn"], count(2, t - 4, 2))
                tt(gl[:, m], g[:, m], hi_view(g[:, m]), ALU.subtract).then_inc(p["gl"], 1)

            def qk_last(t, k):
                eng.wait_ge(a["qk1"], count(4, t, k + 1))
                tt(qkp[:, k % 2, 2], qkr[:], qkp[:, k % 2, 1], ALU.subtract).then_inc(p["qk2"], 1)

            def normalize(t, gi):
                b, g4 = divmod(gi, 4)
                eng.wait_ge(v["cu"], count(8, t - 2, gi + 1))
                if gi == 0:
                    if began(t - 3):
                        eng.wait_ge(pe["ct"], count(2, t - 3, 2))
                    if began(t - 1):
                        eng.wait_ge(pe["xt"], count(2, t - 1, 2))
                dst = cx[:].rearrange("p (q b) d -> p q b d", q=2)[:, :, b, 4 * g4 * HD:4 * g4 * HD + 4 * HD]
                tt(dst.rearrange("p q (e d) -> p q e d", e=4), cu[:, gi % 2].rearrange("p (q e) d -> p q e d", q=2),
                   rs[:, gi % 2].rearrange("p (q e o) -> p q e o", q=2, o=1).broadcast_to([R, 2, 4, HD]),
                   ALU.mult).then_inc(p["cx"], 1)

            def accumulate(t, m):
                eng.wait_ge(a["sq"], count(8, t - 3, m + 1))
                if m == 1:
                    if began(t - 4):
                        eng.wait_ge(pe["ss"], count(1, t - 4, 1))
                    if began(t - 4):
                        eng.wait_ge(v["accl"], count(1, t - 4, 1))
                else:
                    eng.wait_ge(p["acc"], count(7, t - 3, m - 1))
                tt(acc[:], sq[:, 0] if m == 1 else acc[:], sq[:, m % 2], ALU.add).then_inc(p["acc"], 1)

            def step(t, u):
                A, Bm, Cc, Dd = live(t), live(t - 1), live(t - 2), live(t - 3)
                for gi in range(9):
                    if Cc and gi < 8:
                        causal(t, gi)
                    if Cc and gi >= 1:
                        normalize(t, gi - 1)
                for n in range(24):
                    if Dd and n == 0:
                        gelu_lo(t, 0)
                    if Dd and n in (2, 5, 7, 8, 9, 10, 11):
                        accumulate(t, (2, 5, 7, 8, 9, 10, 11).index(n) + 1)
                    if Dd and n in (5, 8):
                        gelu_lo(t, {5: 2, 8: 4}[n])
                    if Cc and n == 5:
                        eng.wait_ge(v["mv2"], count(4, t - 2, 4))
                        if began(t - 3):
                            eng.wait_ge(a["xn2"], count(4, t - 3, 4))
                        apart(eng)
                        var = mv2[:, :, 1:2].rearrange("p j o -> p (j o)")
                        ts(ln2[:, 5], var, EPS, None, ALU.add).then_inc(p["ln2"], 1)
                        tt(ln2[:, 1], var, exps[:, 1], ALU.pow).then_inc(p["ln2"], 1)
                        eng.wait_ge(p["ln2"], count(7, t - 2, 2))
                        tt(ln2[:, 0], ln2[:, 5], exps[:, 0], ALU.pow).then_inc(p["ln2"], 1)
                        eng.wait_ge(p["ln2"], count(7, t - 2, 3))
                        tt(ln2[:, 2], ln2[:, 0], ln2[:, 1], ALU.mult).then_inc(p["ln2"], 1)
                        eng.wait_ge(p["ln2"], count(7, t - 2, 4))
                        apart(eng)
                        ts(ln2[:, 3], ln2[:, 2], RMS_EPS, None, ALU.add).then_inc(p["ln2"], 1)
                        eng.wait_ge(p["ln2"], count(7, t - 2, 5))
                        tt(ln2[:, 6], ln2[:, 3], exps[:, 2], ALU.pow).then_inc(p["ln2"], 1)
                        eng.wait_ge(p["ln2"], count(7, t - 2, 6))
                        tt(ln2[:, 4], ln2[:, 0], ln2[:, 6], ALU.mult).then_inc(p["ln2"], 1)
                    if A and n == 7:
                        eng.wait_ge(v["mv1"], count(4, t, 4))
                        if began(t - 1):
                            eng.wait_ge(a["xn"], count(4, t - 1, 4))
                        apart(eng)
                        ts(rstd1[:, 0], mv1[:, :, 1:2].rearrange("p j o -> p (j o)"), EPS, None,
                           ALU.add).then_inc(p["rstd1"], 1)
                        eng.wait_ge(p["rstd1"], count(2, t, 1))
                        tt(rstd1[:, 1], rstd1[:, 0], exps[:, 0], ALU.pow).then_inc(p["rstd1"], 1)
                    if A and n == 12:
                        eng.wait_ge(a["xn"], count(4, t, 4))
                        hb = h[0:R, u].rearrange("p (j d) -> p j d", j=4)
                        tt(hb, hb, borow[:].rearrange("p (o d) -> p o d", o=1).broadcast_to([R, 4, D]),
                           ALU.add).then_inc(p["bo"], 1)
                    if A and n in (14, 17, 20, 23):
                        qk_last(t, (n - 14) // 3)
                    if Dd and n == 16:
                        eng.wait_ge(v["ss"], count(1, t - 3, 1))
                        if began(t - 4):
                            eng.wait_ge(v["fin"], count(2, t - 4, 2))
                        tt(ssq[:, 1], ssq[:, 0], exps[:, 1], ALU.pow).then_inc(p["ss"], 1)
                        eng.wait_ge(p["ss"], count(3, t - 3, 1))
                        apart(eng)
                        ts(ssq[:, 3], ssq[:, 1], RMS_EPS, None, ALU.add).then_inc(p["ss"], 1)
                        eng.wait_ge(p["ss"], count(3, t - 3, 2))
                        tt(ssq[:, 2], ssq[:, 3], exps[:, 2], ALU.pow).then_inc(p["ss"], 1)

            steps(step, eng)


def kernel(x, txt, L0_tok_W_embed, L0_tok_b_embed, L0_tok_pos_embed, L0_attn_Wq, L0_attn_Wk,
           L0_attn_Wv, L0_attn_Wo, L0_attn_bo, L0_ffn_w_up, L0_ffn_w_down):
    import concourse.bacc as bacc
    from concourse.bass_utils import run_bass_kernel_spmd

    def contiguous(z):
        return np.ascontiguousarray(z)

    we = np.asarray(L0_tok_W_embed).reshape(6, 128, D).transpose(1, 0, 2).reshape(128, 6 * D)

    def interleaved(w):
        return w.reshape(D, 2, 8, HD).transpose(0, 1, 3, 2).reshape(D, D)

    wq, wk, wv, wo = (np.asarray(z).T for z in (L0_attn_Wq, L0_attn_Wk, L0_attn_Wv, L0_attn_Wo))
    wqkvo = np.stack([interleaved(wq), interleaved(wk), wv, wo]).reshape(4, 2, 128, D)
    wqkvo = wqkvo.transpose(2, 0, 1, 3).reshape(128, 8 * D)
    w_upT = np.asarray(L0_ffn_w_up).T.reshape(2, 128, FF).transpose(1, 0, 2).reshape(128, 2 * FF)
    w_downT = np.asarray(L0_ffn_w_down).T.reshape(NFF, 128, D).transpose(1, 0, 2).reshape(128, NFF * D)
    pos = np.asarray(L0_tok_pos_embed)[0]
    pos = np.concatenate([pos, pos[:TXT]]).reshape(2, R, D).transpose(1, 0, 2)
    arrays = {
        "x": contiguous(np.asarray(x)), "txt": contiguous(np.asarray(txt)), "w_embed": contiguous(we),
        "b_embed": contiguous(np.broadcast_to(np.asarray(L0_tok_b_embed), (R, D))),
        "pos": contiguous(pos), "wqkvo": contiguous(wqkvo),
        "bo": contiguous(np.broadcast_to(np.asarray(L0_attn_bo), (R, D))),
        "w_upT": contiguous(w_upT), "w_downT": contiguous(w_downT),
    }
    nc = bacc.Bacc("TRN2", target_bir_lowering=False, num_devices=1)
    args = [nc.dram_tensor(n, z.shape, mybir.dt.from_np(z.dtype), kind="ExternalInput").ap()
            for n, z in arrays.items()]
    out = nc.dram_tensor("out", (B, S, D), F32, kind="ExternalOutput").ap()
    build(nc, *args, out)
    r = run_bass_kernel_spmd(nc, [arrays], core_ids=[0])
    return r.results[0]["out"]
```

```python
from contextlib import ExitStack

import numpy as np
import concourse.bass as bass
from concourse import mybir

ALU = mybir.AluOpType
ACT = mybir.ActivationFunctionType
AX = mybir.AxisListType
F32 = mybir.dt.float32
F32R = mybir.dt.float32r
F16 = mybir.dt.float16
BF16 = mybir.dt.bfloat16

B, C, SIDE, PATCH = 64, 3, 224, 16
NS = SIDE // PATCH
NPATCH = NS * NS
TXT = 32
S = NPATCH + TXT
R = S // 2
RP1 = NPATCH - R
D, H, HD, FF = 256, 16, 16, 1024
NPAIR = B // 2
T2 = 2 * S
TP = 2 * NPATCH
PROWS = 2 * C * NS
PCOLS = PATCH * SIDE
NFF = FF // 128
NXG = [(0, 5), (5, 10), (10, 14)]
HS = H * S
PAD = 16
VW = 1 + 3 * HD
PARTS = [(0, 0), (0, 1), (0, 2), (1, 0), (1, 1), (2, 0)]
KS = len(PARTS) * HD
KM = KS + 3
EPS = 1e-5
RMS_EPS = 1e-8
NEG = -1e30

DENSE = ([("pix", k) for k in range(6)]
         + [("emb", 0), ("x2t", 0), ("x2t", 1), ("up", 0), ("up", 1), ("up", 2), ("emb", 1), ("ht", 0),
            ("ht", 1), ("up", 3), ("up", 4), ("up", 5), ("up", 6), ("up", 7), ("xt", 0), ("xt", 1),
            ("qk", 0), ("qk", 1), ("dn", 0), ("ss", 0), ("v", 0), ("qk", 2), ("v", 1), ("qk", 3),
            ("dn", 1), ("ct", 0), ("ct", 1), ("spare", 0), ("o", 0), ("o", 1)])
QK_AT = {13: 0, 14: 1, 17: 2, 18: 3}
DOWN_AT = {15: (0, 1), 16: (2, 3), 19: (4, 5), 20: (6, 7)}
EMB_AT = {3: (0, 0), 4: (0, 1), 6: (1, 0), 7: (1, 1)}
UP_AT = {5: (0, 1, 2), 9: (3, 4, 5), 10: (6, 7)}
GELU_AT = {5: (0, 1, 2), 9: (3, 4, 5, 6, 7)}
SQ_AT = {6: (0, 1), 7: (2,), 9: (3,), 11: (4,), 12: (5,), 13: (6, 7)}
ACC_AT = {7: (1,), 8: (2,), 10: (3,), 12: (4,), 13: (5,), 14: (6, 7)}
GLV_AT = {7: (1,), 10: (3,), 11: (5,), 12: (6,), 13: (7,)}
GLP_AT = {7: (0,), 8: (2,), 11: (4,)}
PER = {"pix": 6, "emb": 2, "ct": 2, "up": 8, "o": 2, "ht": 2, "xt": 2, "qk": 4, "v": 2, "ss": 1,
       "dn": 2, "x2t": 2}
LAG = {"pix": 0, "emb": 0, "ht": 0, "xt": 0, "qk": 0, "v": 0, "ct": 2, "o": 2, "x2t": 3, "up": 3,
       "ss": 3, "dn": 3}
NDENSE = len(DENSE)
assert NDENSE % 3 == 0


def build(nc, x, txt, w_embed, b_embed, pos, wqkvo, bo, w_upT, w_downT, out):
    qk_scr = nc.dram_tensor("qk_scr", (2, 2, 2, 3, 2, 128, S), BF16, kind="Internal").ap()
    m_scr = nc.dram_tensor("m_scr", (2, 2, 48, S), BF16, kind="Internal").ap()

    with ExitStack() as ctx:
        def sb(name, shape, dt):
            return ctx.enter_context(nc.sbuf_tensor(name, shape, dt))

        def sem(name):
            return ctx.enter_context(nc.semaphore(name))

        ident = sb("ident", [128, 128], F32)
        identb = sb("identb", [128, 128], BF16)
        cmask = sb("cmask", [128, R], BF16)
        onesb = sb("onesb", [128, 2], BF16)
        posb = sb("posb", [R, 2, D], F32)
        borow = sb("borow", [R, D], F32)
        we = [sb("we_hi", [128, 6, D], F32R), sb("we_lo", [128, 6, D], F32R)]
        wa = [sb("wa_hi", [128, 4, 2, D], F32R), sb("wa_lo", [128, 4, 2, D], F32R)]
        wup = sb("wup", [128, 2, FF], BF16)
        wdn = sb("wdn", [128, NFF, D], BF16)
        tern = sb("tern", [128, 8], F32)
        pix = sb("pix", [PROWS, PCOLS], F32)
        pT = [sb("pT_hi", [128, 2, 2 * C * NPATCH], F32R), sb("pT_lo", [128, 2, 2 * C * NPATCH], F32R)]
        hT = sb("hT", [128, 2, TP], F32)
        h = sb("h", [128, 4, 4 * D], F32)
        st1 = sb("st1", [R, 4, 6], F32)
        mv1 = sb("mv1", [R, 4, 2], F32)
        rstd1 = sb("rstd1", [R, 4], F32)
        ve1 = sb("ve1", [R, 4], F32)
        exps = sb("exps", [R, 2, 4], F32)
        aT = [sb("aT_hi", [128, 2, T2], F32R), sb("aT_lo", [128, 2, T2], F32R)]
        qkp = sb("qkp", [128, 2, 3, T2], BF16)
        qkr = sb("qkr", [128, T2], F32)
        vp = sb("vp", [R, 2, 4, H, VW], BF16)
        vr = sb("vr", [R, 2 * D], F32)
        qst = [sb(f"qst{b}", [KM, HS + PAD], BF16) for b in range(2)]
        kst = [sb(f"kst{b}", [KM, HS + PAD], BF16) for b in range(2)]
        mx = sb("mx", [R, 2, 2, H], F32)
        mr = sb("mr", [R, 2, 2, H], F32)
        mp = sb("mp", [R, 2, 2, 3, H], BF16)
        mT = sb("mT", [48, 2, S], BF16)
        PW = 3 * T2 + PAD
        pr = [sb(f"pr{i}", [R, PW], F32) for i in range(2)]
        pl = [sb(f"pl{i}", [R, PW], F16) for i in range(2)]
        cu = sb("cu", [R, 2, 8, HD], F32)
        rs = sb("rs", [R, 2, 8], F32)
        cx = sb("cx", [R, 4, D], F32)
        xn = sb("xn", [R, 4 * D], F32)
        st2 = sb("st2", [R, 4, 6], F32)
        mv2 = sb("mv2", [R, 4, 2], F32)
        nb1 = sb("nb1", [R, 4], F32)
        nb2 = sb("nb2", [R, 4], F32)
        ve2 = sb("ve2", [R, 2, 4], F32)
        pw2 = sb("pw2", [R, 2, 4], F32)
        rm2 = sb("rm2", [R, 3, 4], F32)
        sc2 = sb("sc2", [R, 4], F32)
        xT2 = [sb("xT2_hi", [128, 2, T2], F16), sb("xT2_lo", [128, 2, T2], F16)]
        g = sb("g", [128, NFF, T2], F32)
        gl = sb("gl", [128, NFF, T2], F16)
        sq = sb("sq", [128, 2, T2], F32)
        acc = sb("acc", [128, T2], F32)
        accl = sb("accl", [128, T2], F16)
        ssq = sb("ssq", [R, 4, 4], F32)
        patches = g[0:PROWS].rearrange("p a b -> p (a b)")[:, 0:PCOLS].rearrange(
            "p (h n z) -> p h n z", h=2, n=NS)
        onesf = acc[:, 0:128]
        brow = xn[:, 0:D]

        dense = ctx.enter_context(nc.psum_tensor("dense", [128, 3, 512], F32))
        score = ctx.enter_context(nc.psum_tensor("score", [128, 4, 512], F32))
        pvps = ctx.enter_context(nc.psum_tensor("pvps", [128, 512], F32))

        s_w, s_pix, s_txt = sem("s_w"), sem("s_pix"), sem("s_txt")
        s_qks = [[sem(f"s_qks{u}{i}") for i in range(2)] for u in range(2)]
        s_stack = [[sem(f"s_stack{b}{m}") for m in range(2)] for b in range(2)]
        s_ms = [sem(f"s_ms{b}") for b in range(2)]
        s_mi = [sem(f"s_mi{b}") for b in range(2)]
        s_out = sem("s_out")
        s_apart = sem("s_apart")
        pe = {n: sem("pe_" + n) for n in ["pix", "emb", "ht", "xt", "qk", "v", "s", "st", "pv", "mt",
                                          "ct", "o", "x2t", "up", "ss", "dn", "init"]}
        a = {n: sem("a_" + n) for n in ["ro", "pix", "emb", "xt", "qk0", "qk1", "v0", "v1", "exp", "mt",
                                        "ct", "x2t", "gelu", "sq", "w", "xn", "xn2"]}
        v = {n: sem("v_" + n) for n in ["pix", "h", "st1", "mv1", "nb", "ve1", "ve2", "rm2", "sc2", "rms", "cx", "xt", "qkr", "vr", "v2",
                                        "max", "m0", "mr", "m1", "m2", "pl", "cu", "ct", "h2", "st2",
                                        "mv2", "nb2", "x2t", "gl", "accl", "ss", "fin", "w"]}
        p = {n: sem("p_" + n) for n in ["mask", "pl", "gl", "qk2", "bo", "rstd1", "pw2", "acc", "ss", "w"]}

        def began(pair):
            return not isinstance(pair, int) or pair >= 0

        def count(per, pair, k):
            return (min(pair, NPAIR - 1) if isinstance(pair, int) else pair) * per + k

        def apart(eng):
            eng.sem_inc(s_apart, 1)

        released = {"pix": v["pix"], "emb": a["emb"], "ht": v["h"], "xt": v["xt"], "qk": v["qkr"],
                    "v": v["vr"], "ct": v["ct"], "o": v["h2"], "x2t": v["x2t"], "up": a["gelu"],
                    "ss": v["ss"], "dn": v["fin"]}

        def live(pair):
            return not isinstance(pair, int) or 0 <= pair < NPAIR

        def emptied(pair, name, k):
            m, back = DENSE.index((name, k)) - 3, 0
            while back < 3:
                if m < 0:
                    m, back = m + NDENSE, back + 1
                other, j = DENSE[m]
                if other != "spare":
                    before = pair + (LAG[name] - back - LAG[other])
                    if live(before):
                        return released[other], count(PER[other], before, j + 1)
                m -= 3
            return a["w"], 1

        def unit_at(t, n):
            return (t - 2, n + 9) if n < 15 else (t - 1, n - 15)

        def score_emptied(t, n, keys):
            m, back = 2 * n + (0 if keys else 1) - 4, 0
            while back < 3:
                if m < 0:
                    m, back = m + 48, back + 1
                if m % 2 == 0:
                    pair, q = unit_at(t - back, m // 2)
                    if live(pair):
                        return a["exp"], count(24, pair, q + 1)
                elif live(t - back - 1):
                    return v["max"], count(24, t - back - 1, m // 2 + 1)
                m -= 4
            return a["w"], 1

        def stores(pair, parity, times):
            return ((min(pair, NPAIR - 1) if isinstance(pair, int) else pair) - parity) * 16 + 16 * times

        def bank_of(name, k):
            return dense[:, DENSE.index((name, k)) % 3]

        def hi_view(ap2d):
            return ap2d.bitcast(BF16)[:, 1::2]

        def col(blk, b):
            return b * S + blk * R

        def steps(body, eng):
            for t in range(4):
                body(t, t % 4)
            with eng.Fori(4, NPAIR - 4, 4) as i:
                for j in range(4):
                    body(i + j, j)
            for t in range(NPAIR - 4, NPAIR + 3):
                body(t, t % 4)

        block = ctx.enter_context(nc.Block())

        @block.sync
        def _(sp):
            for i, (dst, src) in enumerate([
                    (g[:].rearrange("p a b -> p (a b)")[:, 0:1536], w_embed),
                    (g[:].rearrange("p a b -> p (a b)")[:, 1536:3584], wqkvo),
                    (h[:, 0:2].rearrange("p a b -> p (a b)"), w_upT),
                    (h[:, 2:4].rearrange("p a b -> p (a b)"), w_downT),
                    (posb[:], pos), (brow, b_embed), (borow[:], bo)]):
                sp.dma_start(dst, src).then_inc(s_w, 16)
            xp = x.rearrange("b c (n q) w -> (b c n) (q w)", q=PATCH)

            def load_pixels(pair):
                sp.dma_start(pix[:], xp[bass.ds(pair * PROWS, PROWS), :]).then_inc(s_pix, 16)

            load_pixels(0)

            def load_stacks(pair, par, b, m):
                if not live(pair):
                    return
                if began(pair - 1):
                    sp.wait_ge(pe["st"], count(24, pair - 1, 12 * b + 6 * m + 6))
                    apart(sp)
                for i in range(2):
                    sp.wait_ge(s_qks[par][i], stores(pair, par, m + 1))
                    apart(sp)
                w = slice(m * HS // 2, (m + 1) * HS // 2)
                for which, st in ((0, qst[b]), (1, kst[b])):
                    for j, parts in enumerate(PARTS):
                        sp.dma_start(st[16 * j:16 * j + 16, w],
                                     qk_scr[par, which, m, parts[which], b].rearrange("(d e) s -> d (e s)", d=HD)
                                     ).then_inc(s_stack[b][m], 16)

            def maxima(pair, par, b):
                if not live(pair):
                    return
                sp.wait_ge(a["mt"], count(2, pair, b + 1))
                sp.dma_start(m_scr[par, b], mT[:, b]).then_inc(s_ms[b], 16)
                sp.wait_ge(s_ms[b], pair * 16 + 16)
                sp.dma_start(qst[b][KS:KM, 0:HS],
                             m_scr[par, b].rearrange("(c e) s -> c (e s)", c=3)).then_inc(s_mi[b], 16)

            def store_parts(pair, par, k):
                if live(pair):
                    sp.wait_ge(p["qk2"], count(4, pair, k + 1))
                    sp.dma_start(qk_scr[par, k % 2, k // 2].rearrange("c b f s -> f c b s"),
                                 qkp[:, k % 2].rearrange("p c (b s) -> p c b s", b=2)
                                 ).then_inc(s_qks[par][k % 2], 16)

            def store_result(pair, hs, blk):
                if live(pair):
                    sp.wait_ge(v["fin"], count(2, pair, blk + 1))
                    sp.dma_start(out[bass.ds(pair * 2, 2), blk * R:blk * R + R].rearrange("b r d -> r b d"),
                                 h[0:R, hs, 2 * D * blk:2 * D * blk + 2 * D].rearrange(
                                     "p (b d) -> p b d", b=2)).then_inc(s_out, 16)

            def step(t, hs):
                u = hs % 2
                if live(t) and (not isinstance(t, int) or t + 1 < NPAIR):
                    sp.wait_ge(a["ro"], count(2, t, 2))
                    load_pixels(t + 1)
                maxima(t - 2, u, 1)
                load_stacks(t - 1, 1 - u, 0, 1)
                if live(t):
                    if isinstance(t, int) and t < 4:
                        sp.wait_ge(v["w"], 11)
                        apart(sp)
                    if began(t - 4):
                        sp.wait_ge(s_out, count(32, t - 4, 32))
                    sp.dma_start(h[RP1:R, hs, 2 * D:4 * D].rearrange("p (b d) -> p b d", b=2),
                                 txt[bass.ds(t * 2, 2)].rearrange("b r d -> r b d")).then_inc(s_txt, 16)
                load_stacks(t - 1, 1 - u, 1, 0)
                maxima(t - 1, 1 - u, 0)
                load_stacks(t - 1, 1 - u, 1, 1)
                store_parts(t, u, 0)
                store_parts(t, u, 1)
                store_result(t - 3, (hs + 1) % 4, 0)
                store_parts(t, u, 2)
                store_parts(t, u, 3)
                load_stacks(t, u, 0, 0)
                store_result(t - 3, (hs + 1) % 4, 1)

            steps(step, sp)
            sp.wait_ge(s_out, 32 * NPAIR)

        @block.tensor
        def _(eng):
            def mm(*args, **kw):
                return nc.tensor.matmul(*args, **kw)

            def three(ps, stat, mov, start, stop):
                mm(ps, stat[0], mov[0], start=start, stop=False)
                mm(ps, stat[0], mov[1], start=False, stop=False)
                return mm(ps, stat[1], mov[0], start=False, stop=stop)

            eng.wait_ge(v["w"], 3)
            mm(dense[:, 0, 0:2], onesf, tern[:, 0:2], start=True, stop=True).then_inc(pe["init"], 1)
            eng.wait_ge(p["w"], 6)
            eng.wait_ge(v["w"], 12)

            def pixels(pair, k):
                eng.wait_ge(*emptied(pair, "pix", k))
                ps = bank_of("pix", k)
                ph, (n0, n1) = k // 3, NXG[k % 3]
                if k % 3 == 0:
                    eng.wait_ge(a["ro"], count(2, pair, ph + 1))
                for i, n in enumerate(range(n0, n1)):
                    last = nc.tensor.transpose(ps[:, i * PROWS:(i + 1) * PROWS],
                                               patches[:, ph, n], ident[0:PROWS, 0:PROWS])
                last.then_inc(pe["pix"], 1)

            def embed(pair, m, ph):
                if ph == 0:
                    eng.wait_ge(*emptied(pair, "emb", m))
                eng.wait_ge(v["pix"], count(6, pair, 3 * ph + 3))
                o = bank_of("emb", m)[:, 0:TP].rearrange("p (b n) -> p b n", b=2)
                for c in range(C):
                    mov = [q[:, ph].rearrange("p (b c n) -> p b c n", b=2, c=C)[:, :, c] for q in pT]
                    stat = [w[:, 2 * c + ph, m * 128:m * 128 + 128] for w in we]
                    last = three(o, stat, mov, ph == 0 and c == 0, ph == 1 and c == 2)
                if ph == 1:
                    last.then_inc(pe["emb"], 1)

            def hidden_rows(pair, blk):
                eng.wait_ge(*emptied(pair, "ht", blk))
                ps = bank_of("ht", blk)
                if blk == 0:
                    eng.wait_ge(a["emb"], count(2, pair, 2))
                w = R if blk == 0 else RP1
                for b in range(2):
                    for m in range(2):
                        c0 = b * NPATCH + blk * R
                        last = nc.tensor.transpose(ps[0:w, b * D + m * 128:b * D + m * 128 + 128],
                                                   hT[:, m, c0:c0 + w], ident[:])
                last.then_inc(pe["ht"], 1)

            def to_columns(pair, name, m, src):
                eng.wait_ge(*emptied(pair, name, m))
                ps = bank_of(name, m)
                for blk in range(2):
                    for b in range(2):
                        c0 = (2 * blk + b) * D + m * 128
                        last = nc.tensor.transpose(ps[:, col(blk, b):col(blk, b) + R], src[:, c0:c0 + 128],
                                                   ident[0:R, 0:R])
                last.then_inc(pe[name], 1)

            def queries_keys(pair, k):
                eng.wait_ge(*emptied(pair, "qk", k))
                ps = bank_of("qk", k)
                if k == 0:
                    eng.wait_ge(v["xt"], count(2, pair, 2))
                for c in range(2):
                    last = three(ps[:, 0:T2], [w[:, k % 2, c, (k // 2) * 128:(k // 2) * 128 + 128] for w in wa],
                                 [q[:, c] for q in aT], c == 0, c == 1)
                last.then_inc(pe["qk"], 1)

            def token_product(pair, name, blk, wi):
                eng.wait_ge(*emptied(pair, name, blk))
                ps = bank_of(name, blk)
                for b in range(2):
                    for c in range(2):
                        last = three(ps[0:R, b * D:b * D + D],
                                     [q[:, c, col(blk, b):col(blk, b) + R] for q in aT],
                                     [w[:, wi, c] for w in wa], c == 0, c == 1)
                last.then_inc(pe[name], 1)

            def up(pair, m):
                eng.wait_ge(*emptied(pair, "up", m))
                ps = bank_of("up", m)
                if m == 0:
                    eng.wait_ge(v["x2t"], count(2, pair, 2))
                for c in range(2):
                    for i in range(2):
                        last = mm(ps[:, 0:T2], wup[:, c, m * 128:m * 128 + 128], xT2[i][:, c],
                                  start=(c == 0 and i == 0), stop=(c == 1 and i == 1))
                last.then_inc(pe["up"], 1)

            def sum_squares(pair):
                eng.wait_ge(*emptied(pair, "ss", 0))
                ps = bank_of("ss", 0)
                eng.wait_ge(v["accl"], count(1, pair, 1))
                for j in range(4):
                    c0 = col(j // 2, j % 2)
                    mm(ps[0:R, j:j + 1], hi_view(acc[:, c0:c0 + R]), onesb[:, 0:1], start=True, stop=False)
                    last = mm(ps[0:R, j:j + 1], accl[:, c0:c0 + R], onesb[:, 0:1], start=False, stop=True)
                last.then_inc(pe["ss"], 1)

            def down(pair, blk, part):
                if part == 0:
                    eng.wait_ge(*emptied(pair, "dn", blk))
                    if blk == 0:
                        eng.wait_ge(v["gl"], count(5, pair, 5))
                        eng.wait_ge(p["gl"], count(3, pair, 3))
                b = part // 2
                c0 = col(blk, b)
                ps = bank_of("dn", blk)[0:R, b * D:b * D + D]
                for m in range(4 * (part % 2), 4 * (part % 2) + 4):
                    mm(ps, hi_view(g[:, m, c0:c0 + R]), wdn[:, m], start=(m == 0), stop=False)
                    last = mm(ps, gl[:, m, c0:c0 + R], wdn[:, m], start=False, stop=(m == NFF - 1))
                if part == 3:
                    last.then_inc(pe["dn"], 1)

            def heads_of(n):
                g4, k = divmod(n, 3)
                return (range(4 * g4, 4 * g4 + 4), False) if k == 2 else (range(4 * g4 + 2 * k, 4 * g4 + 2 * k + 2), True)

            def scores_columns(t, n):
                pair, q = unit_at(t, n)
                if not live(pair):
                    return
                b, k = divmod(q, 12)
                if k == 0:
                    eng.wait_ge(s_mi[b], count(16, pair, 16))
                eng.wait_ge(*score_emptied(t, n, True))
                heads, both = heads_of(k)
                for i, hd in enumerate(heads):
                    c0 = hd * S + (0 if both else R)
                    w = S if both else R
                    rows = R if hd == H // 2 - 1 and not both else 128
                    last = mm(score[0:rows, (2 * n) % 4, i * w:i * w + w], kst[b][0:KM, c0:c0 + rows],
                              qst[b][0:KM, c0:c0 + w], start=True, stop=True)
                last.then_inc(pe["st"], 1)

            def scores_rows(t, n):
                b, k = divmod(n, 12)
                if k in (0, 6):
                    eng.wait_ge(s_stack[b][k // 6], count(192, t - 1, 192))
                eng.wait_ge(*score_emptied(t, n, False))
                heads, both = heads_of(k)
                w = S if both else R
                bank = (2 * n + 1) % 4
                for i, hd in enumerate(heads):
                    c0 = hd * S + (R if both else 0)
                    rows = R if hd == H // 2 - 1 and both else 128
                    mm(score[0:rows, bank, i * w:i * w + w], qst[b][0:KS, c0:c0 + rows],
                       kst[b][0:KS, hd * S:hd * S + w], start=(i == 0), stop=False, skip_group_check=True)
                nh = len(heads)
                o = score[:, bank, 0:T2].rearrange("p (i w) -> p i w", i=nh)[:, :, w - R:w]
                last = mm(o, identb[0:R, :], cmask[0:R].rearrange("p (o w) -> p o w", o=1).broadcast_to([R, nh, R]),
                          start=False, stop=True, skip_group_check=True)
                last.then_inc(pe["s"], 1)

            def weighted_values(pair, par, gi):
                b, g4 = divmod(gi, 4)
                eng.wait_ge(v["pl"], count(8, pair, gi + 1))
                eng.wait_ge(p["pl"], count(8, pair, gi + 1))
                if gi == 0:
                    eng.wait_ge(v["v2"], count(2, pair, 2))
                if gi >= 1:
                    eng.wait_ge(v["cu"], count(8, pair, gi))
                elif began(pair - 1):
                    eng.wait_ge(v["cu"], count(8, pair - 1, 8))
                if gi == 2:
                    eng.wait_ge(a["mt"], count(2, pair, 2))
                if gi == 6 and live(pair + 1):
                    eng.wait_ge(a["mt"], count(2, pair + 1, 1))
                P_, L_ = pr[gi % 2], pl[gi % 2]
                for qb in range(2):
                    for i in range(4):
                        hd = 4 * g4 + i
                        o = pvps[:, (4 * qb + i) * VW:(4 * qb + i) * VW + VW]
                        for kb in range(qb + 1):
                            c0 = i * S + qb * R if kb == 0 else 2 * T2 + i * R
                            val = vp[:, par, 2 * kb + b, hd]
                            mm(o, hi_view(P_[:, c0:c0 + 128]), val, start=(kb == 0), stop=False)
                            last = mm(o[:, 0:1 + 2 * HD], L_[:, c0:c0 + 128], val[:, 0:1 + 2 * HD],
                                      start=False, stop=(kb == qb))
                last.then_inc(pe["pv"], 1)

            def maxima_rows(pair, b):
                eng.wait_ge(v["m2"], count(2, pair, b + 1))
                if b == 0 and began(pair - 1):
                    eng.wait_ge(v["cu"], count(8, pair - 1, 6))
                if b == 1:
                    eng.wait_ge(v["cu"], count(8, pair, 2))
                apart(eng)
                for qb in range(2):
                    last = nc.tensor.transpose(pvps[0:48, 0:256].bitcast(BF16)[:, qb * R:qb * R + R],
                                               mp[:, b, qb].rearrange("p c e -> p (c e)"), identb[0:R, 0:R])
                last.then_inc(pe["mt"], 1)

            def step(t, hs):
                u = hs % 2
                A, Bm, Cc, Dd = live(t), live(t - 1), live(t - 2), live(t - 3)
                for n in range(24):
                    if Bm and n == 13:
                        maxima_rows(t - 1, 0)
                    scores_columns(t, n)
                    if Bm:
                        scores_rows(t, n)
                    if A and n < 3:
                        pixels(t, 2 * n)
                        pixels(t, 2 * n + 1)
                    if Cc and n == 0:
                        maxima_rows(t - 2, 1)
                    if A and n in EMB_AT:
                        embed(t, *EMB_AT[n])
                    if Dd and n == 4:
                        eng.wait_ge(a["xn2"], count(4, t - 3, 4))
                        to_columns(t - 3, "x2t", 0, xn)
                        to_columns(t - 3, "x2t", 1, xn)
                    if A and n == 8:
                        hidden_rows(t, 0)
                        hidden_rows(t, 1)
                    if Dd:
                        for m in UP_AT.get(n, ()):
                            up(t - 3, m)
                    if A and n == 12:
                        eng.wait_ge(a["xn"], count(4, t, 4))
                        to_columns(t, "xt", 0, xn)
                        to_columns(t, "xt", 1, xn)
                    if A and n in QK_AT and n < 15:
                        queries_keys(t, QK_AT[n])
                    if Dd and n == 16:
                        sum_squares(t - 3)
                    if Dd and n in (15, 16, 19):
                        for part in DOWN_AT[n]:
                            down(t - 3, part // 4, part % 4)
                    if A and n in (17, 18):
                        token_product(t, "v", n - 17, 2)
                        queries_keys(t, n - 15)
                    if n % 3 == 1:
                        pair, gi = (t - 2, n // 3 + 2) if n < 18 else (t - 1, n // 3 - 6)
                        if live(pair):
                            weighted_values(pair, u if n < 18 else 1 - u, gi)
                    if Cc and n == 20:
                        eng.wait_ge(v["cx"], count(8, t - 2, 8))
                        to_columns(t - 2, "ct", 0, cx[:].rearrange("p j d -> p (j d)"))
                        to_columns(t - 2, "ct", 1, cx[:].rearrange("p j d -> p (j d)"))
                    if Dd and n == 20:
                        for part in DOWN_AT[n]:
                            down(t - 3, part // 4, part % 4)
                    if Cc and n == 21:
                        eng.wait_ge(v["ct"], count(2, t - 2, 2))
                    if Cc and n in (21, 22):
                        token_product(t - 2, "o", n - 21, 3)

            steps(step, eng)

        @block.scalar
        def _(eng):
            act = nc.scalar.activation
            gf = g[:].rearrange("p a b -> p (a b)")
            eng.wait_ge(s_w, 16 * 7)
            act(we[0][:].rearrange("p a b -> p (a b)"), gf[:, 0:1536], ACT.Copy).then_inc(a["w"], 1)
            act(wa[0][:].rearrange("p a b c -> p (a b c)"), gf[:, 1536:3584], ACT.Copy).then_inc(a["w"], 1)

            def reorder(pair, ph):
                if ph == 0:
                    eng.wait_ge(s_pix, count(16, pair, 16))
                    if began(pair - 4):
                        eng.wait_ge(pe["dn"], count(2, pair - 4, 2))
                    if isinstance(pair, int) and pair == 0:
                        eng.wait_ge(v["w"], 11)
                    if began(pair - 1):
                        eng.wait_ge(pe["pix"], count(6, pair - 1, 6))
                half = PCOLS // 2
                act(patches[:, ph].rearrange("p n (q w) -> p q n w", q=8),
                    pix[:, ph * half:ph * half + half].rearrange("p (q n w) -> p q n w", q=8, n=NS),
                    ACT.Copy).then_inc(a["ro"], 1)

            def pixels_hi(pair, k):
                n0, n1 = NXG[k % 3]
                eng.wait_ge(pe["pix"], count(6, pair, k + 1))
                if k == 0:
                    if began(pair - 1):
                        eng.wait_ge(pe["emb"], count(2, pair - 1, 2))
                src = bank_of("pix", k)[:, 0:(n1 - n0) * PROWS].rearrange("p (n r) -> p r n", r=PROWS)
                dst = pT[0][:, k // 3].rearrange("p (r n) -> p r n", n=NS)[:, :, n0:n1]
                act(dst, src, ACT.Copy).then_inc(a["pix"], 1)

            def hi_part(name, m, dst, pair):
                eng.wait_ge(pe[name], count(2, pair, m + 1))
                act(dst[:, m], bank_of(name, m)[:, 0:T2], ACT.Copy).then_inc(a[name], 1)

            def exponential(t, n):
                pair, q = unit_at(t, n)
                if not live(pair):
                    return
                gi, k = divmod(q, 3)
                if k == 0:
                    if gi >= 2:
                        eng.wait_ge(pe["pv"], count(8, pair, gi - 1))
                    elif began(pair - 1):
                        eng.wait_ge(pe["pv"], count(8, pair - 1, 7 + gi))
                eng.wait_ge(pe["st"], count(24, pair, q + 1))
                act(pr[gi % 2][:, k * T2:k * T2 + T2], score[0:R, (2 * n) % 4, 0:T2], ACT.Exp,
                    scale=float(HD) ** -0.5).then_inc(a["exp"], 1)

            def gelu(pair, m):
                eng.wait_ge(pe["up"], count(8, pair, m + 1))
                if m == 0:
                    if began(pair - 1):
                        eng.wait_ge(pe["dn"], count(2, pair - 1, 2))
                    eng.wait_ge(pe["pix"], count(6, pair, 6))
                act(g[:, m], bank_of("up", m)[:, 0:T2], ACT.Gelu).then_inc(a["gelu"], 1)

            def square(pair, m):
                eng.wait_ge(a["gelu"], count(8, pair, m + 1))
                if m >= 2:
                    eng.wait_ge(p["acc"], count(7, pair, max(1, m - 2)))
                else:
                    if began(pair - 1):
                        eng.wait_ge(p["acc"], count(7, pair - 1, 7))
                act(sq[:, m % 2], g[:, m], ACT.Square).then_inc(a["sq"], 1)

            def part_qk(pair, u, k, i):
                if i == 1:
                    eng.wait_ge(v["qkr"], count(4, pair, k + 1))
                    act(qkp[:, k % 2, 1], qkr[:], ACT.Copy).then_inc(a["qk1"], 1)
                    return
                eng.wait_ge(pe["qk"], count(4, pair, k + 1))
                if k >= 2:
                    eng.wait_ge(s_qks[u][k % 2], stores(pair, u, 1))
                elif began(pair - 1):
                    eng.wait_ge(s_qks[1 - u][k % 2], stores(pair - 1, 1 - u, 2))
                act(qkp[:, k % 2, 0], bank_of("qk", k)[:, 0:T2], ACT.Copy).then_inc(a["qk0"], 1)

            def value_part(pair, u, blk, i):
                dst = vp[:, u, 2 * blk:2 * blk + 2].rearrange("p b e c -> p (b e) c")[:, :, 1 + HD * i:1 + HD * i + HD]
                if i == 0:
                    eng.wait_ge(pe["v"], count(2, pair, blk + 1))
                    if blk == 0:
                        if began(pair - 2):
                            eng.wait_ge(pe["pv"], count(8, pair - 2, 8))
                    act(dst, bank_of("v", blk)[0:R, 0:2 * D].rearrange("p (e c) -> p e c", c=HD),
                        ACT.Copy).then_inc(a["v0"], 1)
                else:
                    eng.wait_ge(v["vr"], count(2, pair, blk + 1))
                    act(dst, vr[:].rearrange("p (e c) -> p e c", c=HD), ACT.Copy).then_inc(a["v1"], 1)

            def normalized(src, dst, scale, bias, s_out_, s_bias, pair):
                eng.wait_ge(s_bias, count(1, pair, 1))
                for j in range(4):
                    act(dst[:, j * D:j * D + D], src[:, j * D:j * D + D], ACT.Identity,
                        bias=bias[:, j:j + 1], scale=scale[:, j:j + 1]).then_inc(s_out_, 1)

            def maxima(pair, b):
                eng.wait_ge(pe["mt"], count(2, pair, b + 1))
                if began(pair - 1):
                    eng.wait_ge(s_ms[b], count(16, pair - 1, 16))
                act(mT[:, b], pvps[0:48, 0:256].bitcast(BF16)[:, 0:S], ACT.Copy).then_inc(a["mt"], 1)

            reorder(0, 0)
            reorder(0, 1)

            def step(t, hs):
                u = hs % 2
                A, Bm, Cc, Dd = live(t), live(t - 1), live(t - 2), live(t - 3)
                following = A and (not isinstance(t, int) or t + 1 < NPAIR)
                for n in range(24):
                    if Bm and n == 13:
                        maxima(t - 1, 0)
                    if A and n == 11:
                        if began(t - 1):
                            eng.wait_ge(pe["xt"], count(2, t - 1, 2))
                        if began(t - 3):
                            eng.wait_ge(pe["x2t"], count(2, t - 3, 2))
                        normalized(h[0:R, hs], xn, rstd1[:], nb1, a["xn"], v["nb"], t)
                    if Dd and n == 3:
                        eng.wait_ge(pe["xt"], count(2, t - 1, 2))
                        if began(t - 4):
                            eng.wait_ge(pe["x2t"], count(2, t - 4, 2))
                        normalized(h[0:R, (hs + 1) % 4], xn, sc2[:], nb2, a["xn2"], v["nb2"], t - 3)
                    exponential(t, n)
                    if A and n - 1 in QK_AT:
                        part_qk(t, u, QK_AT[n - 1], 1)
                    if A and n < 3:
                        pixels_hi(t, 2 * n)
                        pixels_hi(t, 2 * n + 1)
                    if Cc and n == 0:
                        maxima(t - 2, 1)
                    if A and n in (5, 7):
                        m = (n - 5) // 2
                        eng.wait_ge(pe["emb"], count(2, t, m + 1))
                        if m == 0 and began(t - 1):
                            eng.wait_ge(pe["ht"], count(2, t - 1, 2))
                        act(hT[:, m], bank_of("emb", m)[:, 0:TP], ACT.Copy).then_inc(a["emb"], 1)
                    if Dd and n == 4:
                        if began(t - 4):
                            eng.wait_ge(pe["up"], count(8, t - 4, 8))
                        hi_part("x2t", 0, xT2[0], t - 3)
                        hi_part("x2t", 1, xT2[0], t - 3)
                    if A and n == 12:
                        if began(t - 3):
                            eng.wait_ge(pe["o"], count(2, t - 3, 2))
                        if began(t - 1):
                            eng.wait_ge(pe["v"], count(2, t - 1, 2))
                        hi_part("xt", 0, aT[0], t)
                        hi_part("xt", 1, aT[0], t)
                    if A and n in QK_AT:
                        part_qk(t, u, QK_AT[n], 0)
                    if Dd:
                        for m in GELU_AT.get(n, ()):
                            gelu(t - 3, m)
                        for m in SQ_AT.get(n, ()):
                            square(t - 3, m)
                    if A and n == 18:
                        value_part(t, u, 0, 1)
                    if A and n in (17, 18):
                        value_part(t, u, n - 17, 0)
                    if A and n == 19:
                        value_part(t, u, 1, 1)
                    if Cc and n == 20 and A:
                        eng.wait_ge(pe["v"], count(2, t, 2))
                    if Cc and n == 20:
                        hi_part("ct", 0, aT[0], t - 2)
                        hi_part("ct", 1, aT[0], t - 2)
                    if following and n in (22, 23):
                        reorder(t + 1, n - 22)

            steps(step, eng)

        @block.vector
        def _(eng):
            tt, ts = nc.vector.tensor_tensor, nc.vector.tensor_scalar
            gf = g[:].rearrange("p a b -> p (a b)")
            hf, h2f = [h[:, i:i + 2].rearrange("p a b -> p (a b)") for i in (0, 2)]
            eng.memset(onesb[:], 1.0)
            for i, e in enumerate((-0.5, 0.5)):
                eng.memset(exps[:, i], e)
            for b in range(2):
                eng.memset(qst[b][:, HS:], 0.0)
                eng.memset(kst[b][:, HS:], 0.0)
                eng.memset(kst[b][KS:KM, 0:HS], 1.0)
                eng.memset(pr[b][:, 3 * T2:], 0.0)
                eng.memset(pl[b][:, 3 * T2:], 0.0)
            eng.memset(vp[:, :, :, :, 0:1].rearrange("p u j e c -> p (u j e) c"), 1.0)
            eng.memset(onesf, 1.0).then_inc(v["w"], 1)
            eng.wait_ge(s_w, 16 * 7)
            nc.vector.tensor_reduce(tern[:, 0:1], hf, AX.X, ALU.add, apply_absolute_value=True).then_inc(v["w"], 1)
            nc.vector.tensor_reduce(tern[:, 1:2], h2f, AX.X, ALU.add, apply_absolute_value=True).then_inc(v["w"], 1)
            eng.wait_ge(pe["init"], 1)
            ts(tern[:, 2:4], dense[:, 0, 0:2], 0.5 / (D * FF), None, ALU.mult).then_inc(v["w"], 1)
            ts(tern[:, 4:6], dense[:, 0, 0:2], -0.5 / (D * FF), None, ALU.mult).then_inc(v["w"], 1)
            eng.wait_ge(v["w"], 5)
            for i, (src, dst) in enumerate(((hf, wup[:].rearrange("p a b -> p (a b)")),
                                            (h2f, wdn[:].rearrange("p a b -> p (a b)")))):
                below = gf[:, 0:2048]
                if i == 0:
                    eng.wait_ge(a["w"], 2)
                    tt(we[1][:].rearrange("p a b -> p (a b)"), gf[:, 0:1536],
                       we[0][:].bitcast(F32).rearrange("p a b -> p (a b)"), ALU.subtract).then_inc(v["w"], 1)
                    tt(wa[1][:].rearrange("p a b c -> p (a b c)"), gf[:, 1536:3584],
                       wa[0][:].bitcast(F32).rearrange("p a b c -> p (a b c)"), ALU.subtract).then_inc(v["w"], 1)
                    eng.wait_ge(v["w"], 7)
                else:
                    eng.wait_ge(v["w"], 9)
                ts(below, src, tern[:, 4 + i:5 + i], None, ALU.is_lt).then_inc(v["w"], 1)
                if i == 0:
                    eng.wait_ge(v["w"], 8)
                else:
                    eng.wait_ge(v["w"], 10)
                nc.vector.scalar_tensor_tensor(out=dst, in0=src, scalar=tern[:, 2 + i:3 + i], in1=below,
                                               op0=ALU.is_gt, op1=ALU.subtract).then_inc(v["w"], 1)
            tt(posb[:], posb[:], brow.rearrange("p (o d) -> p o d", o=1).broadcast_to([R, 2, D]),
               ALU.add).then_inc(v["w"], 1)
            eng.wait_ge(v["w"], 12)

            def pixels_lo(pair, k):
                n0, n1 = NXG[k % 3]
                eng.wait_ge(a["pix"], count(6, pair, k + 1))
                src = bank_of("pix", k)[:, 0:(n1 - n0) * PROWS].rearrange("p (n r) -> p r n", r=PROWS)
                hi, lo = [q[:, k // 3].rearrange("p (r n) -> p r n", n=NS)[:, :, n0:n1] for q in
                          (pT[0][:].bitcast(F32), pT[1])]
                tt(lo, src, hi, ALU.subtract).then_inc(v["pix"], 1)

            def lo_part(name, m, hi, lo, pair):
                eng.wait_ge(a[name], count(2, pair, m + 1))
                tt(lo[:, m], bank_of(name, m)[:, 0:T2], hi[:, m], ALU.subtract).then_inc(v[name], 1)

            def remainders(pair, gi):
                eng.wait_ge(p["mask"], count(16, pair, 2 * gi + 1))
                if gi >= 2:
                    eng.wait_ge(pe["pv"], count(8, pair, gi - 1))
                else:
                    if began(pair - 1):
                        eng.wait_ge(pe["pv"], count(8, pair - 1, 7 + gi))
                Pb = pr[gi % 2][:, 0:2 * T2]
                tt(pl[gi % 2][:, 0:2 * T2], Pb, hi_view(Pb), ALU.subtract).then_inc(v["pl"], 1)

            def collect(pair, gi):
                eng.wait_ge(pe["pv"], count(8, pair, gi + 1))
                if gi >= 2:
                    eng.wait_ge(v["cx"], count(8, pair, gi - 1))
                else:
                    if began(pair - 1):
                        eng.wait_ge(v["cx"], count(8, pair - 1, 7 + gi))
                bank = pvps[0:R, 0:8 * VW].rearrange("p (e c) -> p e c", c=VW)
                nc.vector.reciprocal(rs[:, gi % 2], bank[:, :, 0:1].rearrange("p e c -> p (e c)"))
                nc.vector.tensor_reduce(cu[:, gi % 2], bank[:, :, 1:VW].rearrange("p e (k d) -> p e d k", k=3),
                                        AX.X, ALU.add).then_inc(v["cu"], 1)

            def gelu_lo(pair, m):
                eng.wait_ge(a["gelu"], count(8, pair, m + 1))
                if m == 1:
                    if began(pair - 1):
                        eng.wait_ge(pe["dn"], count(2, pair - 1, 2))
                tt(gl[:, m], g[:, m], hi_view(g[:, m]), ALU.subtract).then_inc(v["gl"], 1)

            def residual(pair, hs, blk):
                eng.wait_ge(pe["o"], count(2, pair, blk + 1))
                if blk == 0:
                    eng.wait_ge(p["bo"], count(1, pair, 1))
                w = slice(2 * D * blk, 2 * D * blk + 2 * D)
                tt(h[0:R, hs, w], bank_of("o", blk)[0:R, 0:2 * D], h[0:R, hs, w], ALU.add).then_inc(v["h2"], 1)

            def moments(src, st, mv, s_st, s_mv, pair):
                for j in range(4):
                    eng.bn_stats(st[:, j], src[:, j * D:j * D + D]).then_inc(s_st, 1)
                eng.wait_ge(s_st, count(4, pair, 4))
                apart(eng)
                for j in range(4):
                    eng.bn_aggr(mv[:, j], st[:, j]).then_inc(s_mv, 1)

            def maxima_unit(pair, n):
                b, k = divmod(n, 12)
                g4, j = divmod(k, 3)
                eng.wait_ge(pe["s"], count(24, pair, n + 1))
                qb, h0, nh = (0, 4 * g4, 4) if j == 2 else (1, 4 * g4 + 2 * j, 2)
                if n == 0:
                    if began(pair - 1):
                        eng.wait_ge(v["m2"], count(2, pair - 1, 2))
                nc.vector.tensor_reduce(mx[:, b, qb, h0:h0 + nh],
                                        score[0:R, (2 * n + 1) % 4, 0:T2].rearrange("p (i w) -> p i w", i=nh),
                                        AX.X, ALU.max).then_inc(v["max"], 1)

            def maxima_parts(pair, b):
                eng.wait_ge(v["max"], count(24, pair, 12 * b + 12))
                if began(pair - 1):
                    eng.wait_ge(pe["mt"], count(2, pair - 1, b + 1))
                part = [mp[:, b, :, i] for i in range(3)]
                ts(part[0], mx[:, b], -1.0, None, ALU.mult).then_inc(v["m0"], 1)
                eng.wait_ge(v["m0"], count(2, pair, b + 1))
                nc.vector.scalar_tensor_tensor(out=mr[:, b], in0=mx[:, b], scalar=-1.0, in1=part[0],
                                               op0=ALU.mult, op1=ALU.subtract).then_inc(v["mr"], 1)
                eng.wait_ge(v["mr"], count(2, pair, b + 1))
                nc.vector.tensor_copy(part[1], mr[:, b]).then_inc(v["m1"], 1)
                eng.wait_ge(v["m1"], count(2, pair, b + 1))
                tt(part[2], mr[:, b], part[1], ALU.subtract).then_inc(v["m2"], 1)

            def hidden(pair, hs, blk):
                eng.wait_ge(pe["ht"], count(2, pair, blk + 1))
                if blk == 0:
                    if began(pair - 4):
                        eng.wait_ge(s_out, count(32, pair - 4, 32))
                w = R if blk == 0 else RP1
                tt(h[0:w, hs, 2 * D * blk:2 * D * blk + 2 * D].rearrange("p (b d) -> p b d", b=2),
                   bank_of("ht", blk)[0:w].rearrange("p (b d) -> p b d", b=2),
                   posb[0:w, blk].rearrange("p (o d) -> p o d", o=1).broadcast_to([w, 2, D]),
                   ALU.add).then_inc(v["h"], 1)

            def qk_rest(pair, k):
                eng.wait_ge(a["qk0"], count(4, pair, k + 1))
                if k or began(pair - 1):
                    eng.wait_ge(p["qk2"], count(4, pair, k))
                tt(qkr[:], bank_of("qk", k)[:, 0:T2], qkp[:, k % 2, 0], ALU.subtract).then_inc(v["qkr"], 1)

            def value_rest(pair, u, blk, i):
                dst = [vp[:, u, 2 * blk:2 * blk + 2].rearrange("p b e c -> p (b e) c")[:, :, 1 + HD * k:1 + HD * k + HD]
                       for k in range(3)]
                r3 = vr[:].rearrange("p (e c) -> p e c", c=HD)
                if i == 0:
                    eng.wait_ge(a["v0"], count(2, pair, blk + 1))
                    if blk or began(pair - 1):
                        eng.wait_ge(v["v2"], count(2, pair, blk))
                    tt(r3, bank_of("v", blk)[0:R, 0:2 * D].rearrange("p (e c) -> p e c", c=HD), dst[0],
                       ALU.subtract).then_inc(v["vr"], 1)
                else:
                    eng.wait_ge(a["v1"], count(2, pair, blk + 1))
                    tt(dst[2], r3, dst[1], ALU.subtract).then_inc(v["v2"], 1)

            def bias_of(mv, rstd, nb, s_nb):
                nc.vector.scalar_tensor_tensor(out=nb[:], in0=mv[:, :, 0:1].rearrange("p j o -> p (j o)"),
                                               scalar=-1.0, in1=rstd, op0=ALU.mult,
                                               op1=ALU.mult).then_inc(s_nb, 1)

            def normalize(pair, gi):
                b, g4 = divmod(gi, 4)
                eng.wait_ge(v["cu"], count(8, pair, gi + 1))
                if gi == 0:
                    if began(pair - 1):
                        eng.wait_ge(pe["ct"], count(2, pair - 1, 2))
                dst = cx[:].rearrange("p (q b) d -> p q b d", q=2)[:, :, b, 4 * g4 * HD:4 * g4 * HD + 4 * HD]
                tt(dst.rearrange("p q (e d) -> p q e d", e=4), cu[:, gi % 2].rearrange("p (q e) d -> p q e d", q=2),
                   rs[:, gi % 2].rearrange("p (q e o) -> p q e o", q=2, o=1).broadcast_to([R, 2, 4, HD]),
                   ALU.mult).then_inc(v["cx"], 1)

            def scale_of(pair):
                eng.wait_ge(p["pw2"], count(1, pair, 1))
                tt(rm2[:, 0], pw2[:, 0], pw2[:, 1], ALU.mult).then_inc(v["rm2"], 1)
                eng.wait_ge(v["rm2"], count(3, pair, 1))
                ts(rm2[:, 1], rm2[:, 0], RMS_EPS, None, ALU.add).then_inc(v["rm2"], 1)
                eng.wait_ge(v["rm2"], count(3, pair, 2))
                nc.vector.reciprocal(rm2[:, 2], rm2[:, 1]).then_inc(v["rm2"], 1)
                eng.wait_ge(v["rm2"], count(3, pair, 3))
                if began(pair - 1):
                    eng.wait_ge(a["xn2"], count(4, pair - 1, 4))
                tt(sc2[:], pw2[:, 0], rm2[:, 2], ALU.mult).then_inc(v["sc2"], 1)
                eng.wait_ge(v["sc2"], count(1, pair, 1))
                bias_of(mv2, sc2[:], nb2, v["nb2"])

            def rms_of(pair):
                eng.wait_ge(p["ss"], count(1, pair, 1))
                ts(ssq[:, 3], ssq[:, 1], RMS_EPS, None, ALU.add).then_inc(v["rms"], 1)
                eng.wait_ge(v["rms"], count(2, pair, 1))
                nc.vector.reciprocal(ssq[:, 2], ssq[:, 3]).then_inc(v["rms"], 1)
                eng.wait_ge(v["rms"], count(2, pair, 2))

            def final(pair, hs, blk):
                eng.wait_ge(pe["dn"], count(2, pair, blk + 1))
                if blk == 0:
                    rms_of(pair)
                for b in range(2):
                    w = slice((2 * blk + b) * D, (2 * blk + b + 1) * D)
                    last = nc.vector.scalar_tensor_tensor(
                        out=h[0:R, hs, w], in0=bank_of("dn", blk)[0:R, b * D:b * D + D],
                        scalar=ssq[:, 2, 2 * blk + b:2 * blk + b + 1], in1=h[0:R, hs, w],
                        op0=ALU.mult, op1=ALU.add)
                last.then_inc(v["fin"], 1)

            def step(t, hs):
                u = hs % 2
                A, Bm, Cc, Dd = live(t), live(t - 1), live(t - 2), live(t - 3)
                for n in range(24):
                    if Bm:
                        maxima_unit(t - 1, n)
                    if Bm and n in (11, 23):
                        maxima_parts(t - 1, n // 12)
                    if A and n < 3:
                        pixels_lo(t, 2 * n)
                        pixels_lo(t, 2 * n + 1)
                    if Dd and n == 0:
                        eng.wait_ge(v["h2"], count(2, t - 3, 2))
                        if began(t - 4):
                            eng.wait_ge(v["nb2"], count(1, t - 4, 1))
                        moments(h[0:R, (hs + 1) % 4], st2, mv2, v["st2"], v["mv2"], t - 3)
                        eng.wait_ge(v["mv2"], count(4, t - 3, 4))
                        if began(t - 4):
                            eng.wait_ge(p["pw2"], count(1, t - 4, 1))
                        var = mv2[:, :, 1:2].rearrange("p j o -> p (j o)")
                        ts(ve2[:, 0], var, EPS, None, ALU.add)
                        nc.vector.tensor_copy(ve2[:, 1], var).then_inc(v["ve2"], 1)
                    if Dd and n == 2:
                        scale_of(t - 3)
                    if Dd and n == 4:
                        lo_part("x2t", 0, xT2[0], xT2[1], t - 3)
                        lo_part("x2t", 1, xT2[0], xT2[1], t - 3)
                    if A and n == 8:
                        hidden(t, hs, 0)
                        hidden(t, hs, 1)
                    if A and n == 8:
                        eng.wait_ge(v["h"], count(2, t, 2))
                        eng.wait_ge(s_txt, count(16, t, 16))
                        if began(t - 1):
                            eng.wait_ge(v["nb"], count(1, t - 1, 1))
                        moments(h[0:R, hs], st1, mv1, v["st1"], v["mv1"], t)
                        eng.wait_ge(v["mv1"], count(4, t, 4))
                        if began(t - 1):
                            eng.wait_ge(p["rstd1"], count(1, t - 1, 1))
                        ts(ve1[:], mv1[:, :, 1:2].rearrange("p j o -> p (j o)"), EPS, None,
                           ALU.add).then_inc(v["ve1"], 1)
                    if A and n == 9:
                        eng.wait_ge(p["rstd1"], count(1, t, 1))
                        if began(t - 1):
                            eng.wait_ge(a["xn"], count(4, t - 1, 4))
                        bias_of(mv1, rstd1[:], nb1, v["nb"])
                    if Dd and n == 16:
                        eng.wait_ge(pe["ss"], count(1, t - 3, 1))
                        if began(t - 4):
                            eng.wait_ge(p["ss"], count(1, t - 4, 1))
                        ts(ssq[:, 0], bank_of("ss", 0)[0:R, 0:4], 1.0 / FF, None, ALU.mult).then_inc(v["ss"], 1)
                    if A and n == 12:
                        lo_part("xt", 0, aT[0][:].bitcast(F32), aT[1], t)
                        lo_part("xt", 1, aT[0][:].bitcast(F32), aT[1], t)
                    if Dd and n in (17, 21):
                        final(t - 3, (hs + 1) % 4, (n - 17) // 4)
                    if Dd and n == 14:
                        eng.wait_ge(p["acc"], count(7, t - 3, 7))
                        if began(t - 4):
                            eng.wait_ge(pe["ss"], count(1, t - 4, 1))
                        tt(accl[:], acc[:], hi_view(acc[:]), ALU.subtract).then_inc(v["accl"], 1)
                    if A and n in QK_AT:
                        qk_rest(t, QK_AT[n])
                    if Dd:
                        for m in GLV_AT.get(n, ()):
                            gelu_lo(t - 3, m)
                    if A and n == 18:
                        value_rest(t, u, 0, 1)
                    if A and n in (17, 18):
                        value_rest(t, u, n - 17, 0)
                    if A and n == 19:
                        value_rest(t, u, 1, 1)
                    if Cc and n == 20:
                        lo_part("ct", 0, aT[0][:].bitcast(F32), aT[1], t - 2)
                        lo_part("ct", 1, aT[0][:].bitcast(F32), aT[1], t - 2)
                    if Cc and n in (22, 23):
                        residual(t - 2, (hs + 2) % 4, n - 22)
                    if n % 3 == 2:
                        old, gi = (t - 2, n // 3 + 2) if n < 18 else (t - 1, n // 3 - 6)
                        new, gn = (t - 2, n // 3 + 3) if n < 15 else (t - 1, n // 3 - 5)
                        if live(old):
                            collect(old, gi)
                        if live(new):
                            remainders(new, gn)
                        if live(old):
                            normalize(old, gi)

            steps(step, eng)

        @block.gpsimd
        def _(eng):
            tt, ts = nc.gpsimd.tensor_tensor, nc.gpsimd.tensor_scalar
            for idn in (ident, identb):
                eng.memset(idn[:], 0.0).then_inc(p["w"], 1)
            eng.memset(cmask[:], 0.0).then_inc(p["w"], 1)
            eng.wait_ge(p["w"], 3)
            for idn in (ident, identb):
                nc.gpsimd.affine_select(out=idn[:], in_=idn[:], compare_op=ALU.not_equal, fill=1.0, base=0,
                                        pattern=[[-1, 128]], channel_multiplier=1).then_inc(p["w"], 1)
            nc.gpsimd.affine_select(out=cmask[:], in_=cmask[:], compare_op=ALU.is_ge, fill=NEG, base=0,
                                    pattern=[[-1, R]], channel_multiplier=1).then_inc(p["w"], 1)
            eng.wait_ge(v["w"], 1)

            def causal(pair, gi, k):
                Pb = pr[gi % 2]
                blocks = Pb[:, (0, 2 * T2)[k]:(2 * T2, 3 * T2)[k]].rearrange("p (e w) -> p e w", e=4)[:, :, 0:R]
                eng.wait_ge(a["exp"], count(24, pair, 3 * gi + 2 + k))
                apart(eng)
                nc.gpsimd.affine_select(out=blocks, in_=blocks, compare_op=ALU.is_ge, fill=0.0, base=0,
                                        pattern=[[0, 4], [1, R]], channel_multiplier=-1).then_inc(p["mask"], 1)
                if k == 0:
                    return
                eng.wait_ge(p["mask"], count(16, pair, 2 * gi + 2))
                if gi >= 2:
                    eng.wait_ge(pe["pv"], count(8, pair, gi - 1))
                elif began(pair - 1):
                    eng.wait_ge(pe["pv"], count(8, pair - 1, 7 + gi))
                w = slice(2 * T2, 3 * T2)
                tt(pl[gi % 2][:, w], Pb[:, w], hi_view(Pb[:, w]), ALU.subtract).then_inc(p["pl"], 1)

            def gelu_lo(pair, m):
                eng.wait_ge(a["gelu"], count(8, pair, m + 1))
                if m == 0:
                    if began(pair - 1):
                        eng.wait_ge(pe["dn"], count(2, pair - 1, 2))
                tt(gl[:, m], g[:, m], hi_view(g[:, m]), ALU.subtract).then_inc(p["gl"], 1)

            def qk_last(pair, k):
                eng.wait_ge(a["qk1"], count(4, pair, k + 1))
                tt(qkp[:, k % 2, 2], qkr[:], qkp[:, k % 2, 1], ALU.subtract).then_inc(p["qk2"], 1)

            def accumulate(pair, m):
                eng.wait_ge(a["sq"], count(8, pair, m + 1))
                if m == 1:
                    if began(pair - 1):
                        eng.wait_ge(pe["ss"], count(1, pair - 1, 1))
                    if began(pair - 1):
                        eng.wait_ge(v["accl"], count(1, pair - 1, 1))
                else:
                    eng.wait_ge(p["acc"], count(7, pair, m - 1))
                tt(acc[:], sq[:, 0] if m == 1 else acc[:], sq[:, m % 2], ALU.add).then_inc(p["acc"], 1)

            def step(t, hs):
                A, Bm, Cc, Dd = live(t), live(t - 1), live(t - 2), live(t - 3)
                for n in range(24):
                    if Dd:
                        for m in ACC_AT.get(n, ()):
                            accumulate(t - 3, m)
                    if A and n - 1 in QK_AT:
                        qk_last(t, QK_AT[n - 1])
                    if n % 3:
                        pair, gi = (t - 2, n // 3 + 3) if n < 15 else (t - 1, n // 3 - 5)
                        if live(pair):
                            causal(pair, gi, n % 3 - 1)
                    if Dd and n == 1:
                        eng.wait_ge(v["ve2"], count(1, t - 3, 1))
                        if began(t - 4):
                            eng.wait_ge(v["sc2"], count(1, t - 4, 1))
                        tt(pw2[:], ve2[:], exps[:], ALU.pow).then_inc(p["pw2"], 1)
                    if A and n == 8:
                        eng.wait_ge(v["ve1"], count(1, t, 1))
                        if began(t - 1):
                            eng.wait_ge(a["xn"], count(4, t - 1, 4))
                        tt(rstd1[:], ve1[:], exps[:, 0], ALU.pow).then_inc(p["rstd1"], 1)
                    if Dd:
                        for m in GLP_AT.get(n, ()):
                            gelu_lo(t - 3, m)
                    if Dd and n == 16:
                        eng.wait_ge(v["ss"], count(1, t - 3, 1))
                        if began(t - 4):
                            eng.wait_ge(v["rms"], count(2, t - 4, 2))
                        tt(ssq[:, 1], ssq[:, 0], exps[:, 1], ALU.pow).then_inc(p["ss"], 1)
                    if A and n == 20:
                        eng.wait_ge(a["xn"], count(4, t, 4))
                        hb = h[0:R, hs].rearrange("p (j d) -> p j d", j=4)
                        tt(hb, hb, borow[:].rearrange("p (o d) -> p o d", o=1).broadcast_to([R, 4, D]),
                           ALU.add).then_inc(p["bo"], 1)

            steps(step, eng)


def kernel(x, txt, L0_tok_W_embed, L0_tok_b_embed, L0_tok_pos_embed, L0_attn_Wq, L0_attn_Wk,
           L0_attn_Wv, L0_attn_Wo, L0_attn_bo, L0_ffn_w_up, L0_ffn_w_down):
    import concourse.bacc as bacc
    from concourse.bass_utils import run_bass_kernel_spmd

    def contiguous(z):
        return np.ascontiguousarray(z)

    we = np.asarray(L0_tok_W_embed).reshape(6, 128, D).transpose(1, 0, 2).reshape(128, 6 * D)

    def interleaved(w):
        return w.reshape(D, 2, 8, HD).transpose(0, 1, 3, 2).reshape(D, D)

    wq, wk, wv, wo = (np.asarray(z).T for z in (L0_attn_Wq, L0_attn_Wk, L0_attn_Wv, L0_attn_Wo))
    wqkvo = np.stack([interleaved(wq), interleaved(wk), wv, wo]).reshape(4, 2, 128, D)
    wqkvo = wqkvo.transpose(2, 0, 1, 3).reshape(128, 8 * D)
    w_upT = np.asarray(L0_ffn_w_up).T.reshape(2, 128, FF).transpose(1, 0, 2).reshape(128, 2 * FF)
    w_downT = np.asarray(L0_ffn_w_down).T.reshape(NFF, 128, D).transpose(1, 0, 2).reshape(128, NFF * D)
    pos = np.asarray(L0_tok_pos_embed)[0]
    pos = np.concatenate([pos, pos[:TXT]]).reshape(2, R, D).transpose(1, 0, 2)
    arrays = {
        "x": contiguous(np.asarray(x)), "txt": contiguous(np.asarray(txt)), "w_embed": contiguous(we),
        "b_embed": contiguous(np.broadcast_to(np.asarray(L0_tok_b_embed), (R, D))),
        "pos": contiguous(pos), "wqkvo": contiguous(wqkvo),
        "bo": contiguous(np.broadcast_to(np.asarray(L0_attn_bo), (R, D))),
        "w_upT": contiguous(w_upT), "w_downT": contiguous(w_downT),
    }
    nc = bacc.Bacc("TRN2", target_bir_lowering=False, num_devices=1)
    args = [nc.dram_tensor(n, z.shape, mybir.dt.from_np(z.dtype), kind="ExternalInput").ap()
            for n, z in arrays.items()]
    out = nc.dram_tensor("out", (B, S, D), F32, kind="ExternalOutput").ap()
    build(nc, *args, out)
    r = run_bass_kernel_spmd(nc, [arrays], core_ids=[0])
    return r.results[0]["out"]
```
